# Optimizing a Trainium2 kernel written in Bass

```python
import numpy as np
import jax
import jax.numpy as jnp

def _softmax(x, axis=-1):
    return jax.nn.softmax(x, axis=axis)

def _gelu(x):
    return jax.nn.gelu(x, approximate=True)

def _silu(x):
    return jax.nn.silu(x)

def _sigmoid(x):
    return jax.nn.sigmoid(x)

def _layernorm(x, axis=-1, eps=1e-05):
    m = jnp.mean(x, axis=axis, keepdims=True)
    v = jnp.var(x, axis=axis, keepdims=True)
    return (x - m) / jnp.sqrt(v + eps)

def _scatter_add(tgt, idx, src, axis=0):
    return tgt.at[idx].add(src)

def _segment_sum(src, seg, n):
    return jax.ops.segment_sum(src, seg, n)
kernel_name = 'mk_vit_tower_cls_d1_tok_img1024_r4_9b5d0f'

def setup_inputs(seed: int=0):
    np.random.seed(seed)
    _w = jnp.asarray

    def _rec_inputs():
        import jax
        import jax.numpy as jnp
        _rk = jax.random.key(seed)
        x = -0.000222058 + 0.999998 * jax.random.normal(jax.random.fold_in(_rk, 1), (32, 3, 64, 64), jnp.float32)
        cls_tok = 0.02 * jax.random.normal(jax.random.fold_in(_rk, 5), (1, 1, 256), jnp.float32)
        return (x, cls_tok)
    x, cls_tok = _rec_inputs()

    def _L0_tok_setup():
        import jax, jax.numpy as jnp
        import numpy as np
        IMG, PS, C, OUT = (64, 16, 3, 256)
        NP = IMG // PS
        IN_FEAT = C * PS * PS
        key = jax.random.key(seed)
        k1, k2, k3, k4 = jax.random.split(key, 4)
        x = jax.random.normal(k1, (128, C, IMG, IMG), dtype=jnp.float32)
        W = jax.random.normal(k2, (OUT, IN_FEAT), dtype=jnp.float32) / np.sqrt(IN_FEAT)
        b = jax.random.normal(k3, (OUT,), dtype=jnp.float32) * 0.01
        pos_emb = jax.random.normal(k4, (NP * NP, OUT), dtype=jnp.float32)
        return {'x': x, 'W': W, 'b': b, 'pos_emb': pos_emb}
    _L0_tok_all = _L0_tok_setup()
    _L0_tok_in = {k: v for k, v in _L0_tok_all.items() if k in ('W', 'b', 'pos_emb')}
    del _L0_tok_all

    def _L0_attn_setup():
        import jax, jax.numpy as jnp
        import numpy as np
        import math
        N_HEAD = 16
        N_KV_HEAD = 4
        HEAD_DIM = 64
        ROPE_THETA = 10000.0

        def _rope_cache(T, D, dtype):
            inv_freq = 1.0 / ROPE_THETA ** (jnp.arange(0, D, 2, dtype=dtype) / D)
            t = jnp.arange(T, dtype=dtype)
            freqs = jnp.einsum('i,j->ij', t, inv_freq)
            return (jnp.cos(freqs)[None, None], jnp.sin(freqs)[None, None])

        def _apply_rope(x, cos, sin):
            x1 = x[..., ::2]
            x2 = x[..., 1::2]
            return jnp.concatenate([x1 * cos - x2 * sin, x1 * sin + x2 * cos], axis=-1)
        key = jax.random.key(seed)
        k0, k1, k2, k3, k4 = jax.random.split(key, 5)
        B, T, C = (4, 512, 256)
        scale = 0.02
        return {'x': jax.random.normal(k0, (B, T, C), dtype=jnp.float32), 'Wq': jax.random.normal(k1, (C, N_HEAD * HEAD_DIM), dtype=jnp.float32) * scale, 'Wk': jax.random.normal(k2, (C, N_KV_HEAD * HEAD_DIM), dtype=jnp.float32) * scale, 'Wv': jax.random.normal(k3, (C, N_KV_HEAD * HEAD_DIM), dtype=jnp.float32) * scale, 'Wo': jax.random.normal(k4, (N_HEAD * HEAD_DIM, C), dtype=jnp.float32) * scale}
    _L0_attn_all = _L0_attn_setup()
    _L0_attn_in = {k: v for k, v in _L0_attn_all.items() if k in ('Wq', 'Wk', 'Wv', 'Wo')}
    del _L0_attn_all

    def _L0_ffn_setup():
        import jax, jax.numpy as jnp
        import numpy as np
        HIDDEN = 256
        INNER = 1024

        def _weight_quant(w):
            scale = 1.0 / jnp.clip(jnp.mean(jnp.abs(w)), 1e-05)
            wq = jnp.clip(jnp.round(w * scale), -1.0, 1.0) / scale
            return w + jax.lax.stop_gradient(wq - w)

        def _act_quant(x):
            scale = 127.0 / jnp.clip(jnp.max(jnp.abs(x), axis=-1, keepdims=True), 1e-05)
            xq = jnp.clip(jnp.round(x * scale), -128.0, 127.0) / scale
            return x + jax.lax.stop_gradient(xq - x)

        def _bitlinear(x, w):
            return jnp.einsum('bsi,oi->bso', _act_quant(x), _weight_quant(w))
        key = jax.random.key(seed)
        k0, k1, k2, k3 = jax.random.split(key, 4)
        x = jax.random.normal(k0, (4, 512, HIDDEN), dtype=jnp.float32)
        w_gate = jax.random.normal(k1, (INNER, HIDDEN), dtype=jnp.float32) / np.sqrt(HIDDEN)
        w_up = jax.random.normal(k2, (INNER, HIDDEN), dtype=jnp.float32) / np.sqrt(HIDDEN)
        w_down = jax.random.normal(k3, (HIDDEN, INNER), dtype=jnp.float32) / np.sqrt(INNER)
        return {'x': x, 'w_gate': w_gate, 'w_up': w_up, 'w_down': w_down}
    _L0_ffn_all = _L0_ffn_setup()
    _L0_ffn_in = {k: v for k, v in _L0_ffn_all.items() if k in ('w_gate', 'w_up', 'w_down')}
    del _L0_ffn_all
    return {'x': x, 'cls_tok': cls_tok, 'L0_tok_W': _L0_tok_in['W'], 'L0_tok_b': _L0_tok_in['b'], 'L0_tok_pos_emb': _L0_tok_in['pos_emb'], 'L0_attn_Wq': _L0_attn_in['Wq'], 'L0_attn_Wk': _L0_attn_in['Wk'], 'L0_attn_Wv': _L0_attn_in['Wv'], 'L0_attn_Wo': _L0_attn_in['Wo'], 'L0_ffn_w_gate': _L0_ffn_in['w_gate'], 'L0_ffn_w_up': _L0_ffn_in['w_up'], 'L0_ffn_w_down': _L0_ffn_in['w_down']}

def reference(x, cls_tok, L0_tok_W, L0_tok_b, L0_tok_pos_emb, L0_attn_Wq, L0_attn_Wk, L0_attn_Wv, L0_attn_Wo, L0_ffn_w_gate, L0_ffn_w_up, L0_ffn_w_down):
    import jax
    import jax.numpy as jnp

    def _L0_tok_ref(x, W, b, pos_emb):
        import jax, jax.numpy as jnp
        import numpy as np
        IMG, PS, C, OUT = (64, 16, 3, 256)
        NP = IMG // PS
        IN_FEAT = C * PS * PS
        B = x.shape[0]
        p = x.reshape(B, C, NP, PS, NP, PS).transpose(0, 1, 2, 4, 3, 5)
        p = p.transpose(0, 2, 3, 1, 4, 5)
        p = p.reshape(B, NP * NP, IN_FEAT)
        out = jnp.einsum('bnf,of->bno', p, W) + b + pos_emb
        return out

    def _L0_attn_ref(x, Wq, Wk, Wv, Wo):
        import jax, jax.numpy as jnp
        import numpy as np
        import math
        N_HEAD = 16
        N_KV_HEAD = 4
        HEAD_DIM = 64
        ROPE_THETA = 10000.0

        def _rope_cache(T, D, dtype):
            inv_freq = 1.0 / ROPE_THETA ** (jnp.arange(0, D, 2, dtype=dtype) / D)
            t = jnp.arange(T, dtype=dtype)
            freqs = jnp.einsum('i,j->ij', t, inv_freq)
            return (jnp.cos(freqs)[None, None], jnp.sin(freqs)[None, None])

        def _apply_rope(x, cos, sin):
            x1 = x[..., ::2]
            x2 = x[..., 1::2]
            return jnp.concatenate([x1 * cos - x2 * sin, x1 * sin + x2 * cos], axis=-1)
        B, T, C = x.shape
        H, Hkv, D = (N_HEAD, N_KV_HEAD, HEAD_DIM)
        q = (x @ Wq).reshape(B, T, H, D).transpose(0, 2, 1, 3)
        k = (x @ Wk).reshape(B, T, Hkv, D).transpose(0, 2, 1, 3)
        v = (x @ Wv).reshape(B, T, Hkv, D).transpose(0, 2, 1, 3)
        rep = H // Hkv
        k = jnp.repeat(k, rep, axis=1)
        v = jnp.repeat(v, rep, axis=1)
        cos, sin = _rope_cache(T, D, x.dtype)
        q = _apply_rope(q, cos, sin)
        k = _apply_rope(k, cos, sin)
        att = jnp.einsum('bhtd,bhsd->bhts', q, k) / math.sqrt(D)
        mask = jnp.tril(jnp.ones((T, T), dtype=bool))
        att = jnp.where(mask, att, -jnp.inf)
        att = jax.nn.softmax(att, axis=-1)
        y = jnp.einsum('bhts,bhsd->bhtd', att, v)
        y = y.transpose(0, 2, 1, 3).reshape(B, T, H * D)
        return y @ Wo

    def _L0_ffn_ref(x, w_gate, w_up, w_down):
        import jax, jax.numpy as jnp
        import numpy as np
        HIDDEN = 256
        INNER = 1024

        def _weight_quant(w):
            scale = 1.0 / jnp.clip(jnp.mean(jnp.abs(w)), 1e-05)
            wq = jnp.clip(jnp.round(w * scale), -1.0, 1.0) / scale
            return w + jax.lax.stop_gradient(wq - w)

        def _act_quant(x):
            scale = 127.0 / jnp.clip(jnp.max(jnp.abs(x), axis=-1, keepdims=True), 1e-05)
            xq = jnp.clip(jnp.round(x * scale), -128.0, 127.0) / scale
            return x + jax.lax.stop_gradient(xq - x)

        def _bitlinear(x, w):
            return jnp.einsum('bsi,oi->bso', _act_quant(x), _weight_quant(w))
        gate = jax.nn.silu(_bitlinear(x, w_gate))
        up = _bitlinear(x, w_up)
        return _bitlinear(gate * up, w_down)
    h = _L0_tok_ref(x, L0_tok_W, L0_tok_b, L0_tok_pos_emb)
    h = jnp.concatenate([jnp.broadcast_to(cls_tok, (h.shape[0], 1, h.shape[2])), h], axis=1)
    h = h + _L0_attn_ref(_layernorm(h, axis=-1), L0_attn_Wq, L0_attn_Wk, L0_attn_Wv, L0_attn_Wo)
    h = h + _L0_ffn_ref(_layernorm(h, axis=-1), L0_ffn_w_gate, L0_ffn_w_up, L0_ffn_w_down)
    return h

_drawn_inputs = setup_inputs


def setup_inputs(seed=0):
    import zlib

    import numpy as np

    out = dict(_drawn_inputs(seed))
    spreads = {}
    factors = {'L0_tok_b': 7.421, 'L0_attn_Wq': 8.0, 'L0_attn_Wk': 8.0}
    for name, (base, spread) in spreads.items():
        noise = np.random.default_rng([zlib.crc32(name.encode()), seed]).standard_normal(out[name].shape)
        drawn = base * np.exp(spread * noise) if base else spread * noise
        out[name] = jnp.asarray(drawn.astype(out[name].dtype))
    for name, factor in factors.items():
        out[name] = (out[name] * factor).astype(out[name].dtype)
    return out
```

```python
from contextlib import ExitStack

import concourse.bass as bass
from concourse import mybir

ALU = mybir.AluOpType
ACT = mybir.ActivationFunctionType
F32 = mybir.dt.float32
BF16 = mybir.dt.bfloat16
AX_X = mybir.AxisListType.X

P = 128
B = 32
N = 16
S = N + 1
C = 256
CC = C // P
IN_FEAT = 768
FC = IN_FEAT // P
G, R, D = 4, 4, 64
HD = D // 2
INNER = 1024
IC = INNER // P
TOK = B * N
TILES = TOK // P
TI = P // N
PAIRS = TI // 2
HALF = TOK // 2
GK = G * S
EPS = 1e-5
MASKED = -1e30
MAGIC = 1.5 * 2.0 ** 23
QMAX = 127.0
SCALE = float(D) ** -0.5


def build(nc, xT, w_tok, tok_b, pos, cls_tok, wq, wk, wv, wo, w_gate, w_up, w_down,
          cos_t, sin_t, mask_t, eye_f, out):
    with ExitStack() as ctx:
        def sb(name, shape, dt=F32):
            return ctx.enter_context(nc.sbuf_tensor(name, shape, dt))

        def sem(name):
            return ctx.enter_context(nc.semaphore(name))

        x_sb = sb("x_sb", [P, FC, TOK])
        wtok_sb = sb("wtok_sb", [P, FC, C])
        b_sb = sb("b_sb", [P, C])
        pos_sb = sb("pos_sb", [P, C])
        posb = sb("posb", [P, C])
        wq_sb = sb("wq_sb", [P, CC, R, 2, P])
        wk_sb = sb("wk_sb", [P, CC, 2, P])
        wv_sb = sb("wv_sb", [P, CC, C])
        wo_sb = sb("wo_sb", [P, 2, R, C])
        wo_sum = sb("wo_sum", [P, 2, C])
        raw = {n: sb(f"raw_{n}", [P, 2 * INNER]) for n in ("gate", "up", "down")}
        tern = {n: sb(f"tern_{n}", [P, 2 * INNER], BF16) for n in ("gate", "up", "down")}
        below = sb("below", [P, 2 * INNER], BF16)
        abs_junk = below
        cos_sb = sb("cos_sb", [P, N])
        sin_sb = sb("sin_sb", [P, N])
        mask_sb = sb("mask_sb", [P, S])
        eyef = sb("eyef", [P, P])
        eyeb = sb("eyeb", [P, P], BF16)
        ones = sb("ones", [P, P])
        mhalf = sb("mhalf", [P, 1])
        h_sb = sb("h_sb", [P, TILES + 1, C])
        y_sb = sb("y_sb", [P, 2, C])
        yT = sb("yT", [P, CC, TOK + 1])
        stats = sb("stats", [P, TILES + 1, 2, 8])
        rstd = sb("rstd", [P, TILES + 1, 2, 2])
        rc = sb("rc", [P, 2, 2, HALF])
        rs = sb("rs", [P, 2, 2, HALF])
        qr = sb("qr", [P, 2, B, R, N])
        kb = sb("kb", [P, 2, B, GK])
        kcls = sb("kcls", [P, 2])
        v_sb = sb("v_sb", [P, TILES + 1, C])
        vb = sb("vb", [GK, B, C])
        vT = sb("vT", [P, 2])
        sc = sb("sc", [P, 2, PAIRS * GK])
        ex = sb("ex", [P, 2, PAIRS * GK])
        smax = sb("smax", [P, 2, PAIRS * G])
        ssum = sb("ssum", [P, 2, PAIRS * G])
        srec = sb("srec", [P, 2, PAIRS * G])
        pT = sb("pT", [GK, 2, PAIRS * P])
        oT = sb("oT", [P, 2, 2, R, P])
        asum = sb("asum", [P, 4])
        wm = sb("wm", [P, 3])
        thr = sb("thr", [P, 3])
        nthr = sb("nthr", [P, 3])
        wdq = sb("wdq", [P, 3])
        q1 = sb("q1", [P, TILES + 1, 8])
        dx = sb("dx", [P, 2, C])
        xm = sb("xm", [P, 2, C])
        xq = sb("xq", [P, 2, C], BF16)
        xqT = sb("xqT", [P, 2, CC, P], BF16)
        sg = x_sb[:, 0:4, :].rearrange("p (a b) n -> p a (b n)", a=2)
        g2 = wq_sb[:, :, :, :, :].rearrange("p c r j m -> p c (r j m)")
        g2m = x_sb[:, 4:6, :].rearrange("p a n -> p (a n)")
        g2q = sb("g2q", [P, 2, INNER], BF16)
        g2T = sb("g2T", [P, 2, IC, P], BF16)
        o_sb = h_sb
        v_dram = nc.dram_tensor("v_scratch", [TOK + 1, C], F32, kind="Internal").ap()

        bank = [ctx.enter_context(nc.psum_tensor(f"bank{i}", [P, 512], F32)) for i in range(8)]
        bankb = [b[:, :].bitcast(BF16) for b in bank]

        ld_cls, ld_pos, ld_b, ld_eyef, ld_tab = (sem(n) for n in (
            "ld_cls", "ld_pos", "ld_b", "ld_eyef", "ld_tab"))
        ld_x = [sem(f"ld_x{c}") for c in range(FC)]
        ld_wk, ld_wv, ld_wo, ld_gate, ld_up, ld_down = (sem(n) for n in (
            "ld_wk", "ld_wv", "ld_wo", "ld_gate", "ld_up", "ld_down"))
        ld_wq = [sem(f"ld_wq{c}") for c in range(2)]
        v_stored = sem("v_stored")
        vb_loaded = [sem(f"vb_loaded{h}") for h in range(3)]
        stored = sem("stored")
        const_ready, kb_zero, vb_zero = sem("const_ready"), sem("kb_zero"), sem("vb_zero")
        embedded, posb_ready, h_ready = sem("embedded"), sem("posb_ready"), sem("h_ready")
        dve_link, pool_link, act_link = sem("dve_link"), sem("pool_link"), sem("act_link")
        var_ready, rstd_ready, y_ready = sem("var_ready"), sem("rstd_ready"), sem("y_ready")
        yT_psum, yT_ready = sem("yT_psum"), sem("yT_ready")
        v_psum, v_ready = sem("v_psum"), sem("v_ready")
        kc_psum, kc_copied = sem("kc_psum"), sem("kc_copied")
        vT_psum, vT_ready = sem("vT_psum"), sem("vT_ready")
        proj_psum, proj_read, roped = sem("proj_psum"), sem("proj_read"), sem("roped")
        kcls_placed = sem("kcls_placed")
        abs_done, tot_psum, wm_ready, tern_ready = (sem(n) for n in (
            "abs_done", "tot_psum", "wm_ready", "tern_ready"))
        below_ready = sem("below_ready")
        wo_summed = sem("wo_summed")
        s_psum, s_read, smax_ready, shifted, exp_done = (sem(n) for n in (
            "s_psum", "s_read", "smax_ready", "shifted", "exp_done"))
        srec_ready, probs_ready, pT_psum, pT_ready = (sem(n) for n in (
            "srec_ready", "probs_ready", "pT_psum", "pT_ready"))
        o_psum, oT_ready, a_psum, h1_ready = (sem(n) for n in (
            "o_psum", "oT_ready", "a_psum", "h1_ready"))
        var2_ready, rstd2_ready, xq_ready, xqT_psum, xqT_ready = (sem(n) for n in (
            "var2_ready", "rstd2_ready", "xq_ready", "xqT_psum", "xqT_ready"))
        gu_psum, sg_ready, g2_ready, g2m_ready, g2q_ready, g2T_psum, g2T_ready = (sem(n) for n in (
            "gu_psum", "sg_ready", "g2_ready", "g2m_ready", "g2q_ready", "g2T_psum", "g2T_ready"))
        scale1_ready = sem("scale1_ready")
        d_psum, out_ready = sem("d_psum"), sem("out_ready")

        block = ctx.enter_context(nc.Block())

        def rows(t):
            return 1 if t == 0 else P

        def tcols(t):
            return slice(TOK, TOK + 1) if t == 0 else slice((t - 1) * P, t * P)

        ALL = range(TILES + 1)
        PATCH = range(1, TILES + 1)

        @block.sync
        def _(sp):
            sp.dma_start(h_sb[0:1, 0, :], cls_tok).then_inc(ld_cls, 16)
            sp.dma_start(eyef[:, :], eye_f).then_inc(ld_eyef, 16)
            for c in range(FC):
                sp.dma_start(x_sb[:, c, :], xT[c]).then_inc(ld_x[c], 16)
                sp.dma_start(wtok_sb[:, c, :], w_tok[c]).then_inc(ld_x[c], 16)
            sp.dma_start(pos_sb[:, :], pos).then_inc(ld_pos, 16)
            sp.dma_start(b_sb[:, :], tok_b.broadcast_to([P, C])).then_inc(ld_b, 16)
            sp.dma_start(wv_sb[:, :, :], wv).then_inc(ld_wv, 16)
            sp.dma_start(wk_sb[:, :, :, :], wk).then_inc(ld_wk, 16)
            sp.dma_start(cos_sb[:, :], cos_t).then_inc(ld_tab, 16)
            sp.dma_start(sin_sb[:, :], sin_t).then_inc(ld_tab, 16)
            sp.dma_start(mask_sb[:, :], mask_t).then_inc(ld_tab, 16)
            for c in range(2):
                sp.dma_start(wq_sb[:, :, 2 * c:2 * c + 2, :, :], wq[:, :, 2 * c:2 * c + 2, :, :])\
                    .then_inc(ld_wq[c], 16)
            sp.dma_start(wo_sb[:, :, :, :], wo).then_inc(ld_wo, 16)
            sp.dma_start(raw["gate"][:, :], w_gate).then_inc(ld_gate, 16)
            sp.dma_start(raw["up"][:, :], w_up).then_inc(ld_up, 16)
            sp.dma_start(raw["down"][:, :], w_down).then_inc(ld_down, 16)

            for t in ALL:
                sp.wait_ge(v_ready, t + 1)
                dst = v_dram[TOK:TOK + 1, :] if t == 0 else v_dram[(t - 1) * P:t * P, :]
                sp.dma_start(dst, v_sb[0:rows(t), t, :]).then_inc(v_stored, 16)
            sp.wait_ge(vb_zero, 2)
            sp.wait_ge(v_stored, 16 * (TILES + 1))
            vg = v_dram[0:TOK, :].rearrange("(b n) (g d) -> g n b d", n=N, g=G)
            for g in range(G):
                sp.dma_start(vb[g * S:g * S + 1, :, g * D:(g + 1) * D],
                             v_dram[TOK:TOK + 1, g * D:(g + 1) * D].unsqueeze(1)
                             .broadcast_to([1, B, D])).then_inc(vb_loaded[0], 16)
            for half in range(2):
                bs = slice(half * B // 2, (half + 1) * B // 2)
                for g in range(G):
                    sp.dma_start(vb[g * S + 1:(g + 1) * S, bs, g * D:(g + 1) * D],
                                 vg[g, :, bs, :]).then_inc(vb_loaded[1 + half], 16)
            for t in ALL:
                sp.wait_ge(out_ready, t + 1)
                if t == 0:
                    sp.dma_start(out[:, 0:1, :].rearrange("b s c -> s b c"),
                                 o_sb[0:1, 0, :].unsqueeze(1).broadcast_to([1, B, C]))\
                        .then_inc(stored, 16)
                else:
                    for b in range(TI):
                        sp.dma_start(out[(t - 1) * TI + b, 1:S, :],
                                     o_sb[b * N:(b + 1) * N, t, :]).then_inc(stored, 16)
            sp.wait_ge(stored, 16 * (1 + TILES * TI))

        @block.tensor
        def _(pe):
            def transpose_y(t):
                pe.wait_ge(y_ready, t + 1)
                if t >= 2:
                    pe.wait_ge(yT_ready, t - 1)
                n = rows(t)
                for c in range(CC):
                    last = nc.tensor.transpose(bank[4 + t % 2][:, c * P:c * P + n],
                                               y_sb[0:n, t % 2, c * P:(c + 1) * P], eyef[0:n, 0:n])
                last.then_inc(yT_psum, 1)

            def values(t):
                pe.wait_ge(yT_ready, t + 1)
                if t >= 2:
                    pe.wait_ge(v_ready, t - 1)
                for c in range(CC):
                    last = nc.tensor.matmul(bank[6 + t % 2][0:rows(t), 0:C], yT[:, c, tcols(t)],
                                            wv_sb[:, c, :], start=c == 0, stop=c == CC - 1)
                last.then_inc(v_psum, 1)

            def project(s):
                half, r = divmod(s, R + 1)
                w = wk_sb[:, :, :, :] if r == 0 else wq_sb[:, :, r - 1, :, :]
                if s < 4:
                    pe.wait_ge(h_ready, s + 1)
                else:
                    pe.wait_ge(proj_read, s - 3)
                pe.wait_ge(yT_ready, 3 + 2 * half)
                for j in range(2):
                    for c in range(CC):
                        last = nc.tensor.matmul(bank[s % 4][:, j * HALF:(j + 1) * HALF], w[:, c, j, :],
                                                yT[:, c, half * HALF:(half + 1) * HALF],
                                                start=c == 0, stop=c == CC - 1)
                last.then_inc(proj_psum, 1)

            def scores(t):
                pe.wait_ge(roped, 5 if t <= 2 else 10)
                if t == 1:
                    pe.wait_ge(kcls_placed, 1)
                    pe.wait_ge(yT_ready, 4)
                elif t == 2:
                    pe.wait_ge(yT_ready, 5)
                else:
                    pe.wait_ge(s_read, t - 2)
                for b in range(TI):
                    img, row = (t - 1) * TI + b, b % 2 * D
                    for j in range(2):
                        last = nc.tensor.matmul(
                            bank[4 + t % 2][row:row + D, b // 2 * GK:(b // 2 + 1) * GK],
                            qr[:, j, img, :, :].rearrange("p r n -> p (r n)"), kb[:, j, img, :],
                            start=j == 0, stop=j == 1)
                last.then_inc(s_psum, 1)

            def transpose_probs(t):
                pe.wait_ge(probs_ready, t)
                if t >= 2:
                    pe.wait_ge(pT_ready, t - 1)
                else:
                    pe.wait_ge(v_ready, 5)
                for pr in range(PAIRS):
                    last = nc.tensor.transpose(bank[6][0:GK, pr * P:(pr + 1) * P],
                                               ex[:, t % 2, pr * GK:(pr + 1) * GK], eyef[:, :])
                last.then_inc(pT_psum, 1)

            def mix(t):
                pe.wait_ge(pT_ready, t)
                if t == 1:
                    pe.wait_ge(vb_loaded[0], 16 * G)
                if t % 2:
                    pe.wait_ge(vb_loaded[1 + t // 2], 16 * G)
                pe.wait_ge(proj_read, 10)
                if t >= 3:
                    pe.wait_ge(oT_ready, t - 2)
                for gp in range(2):
                    for b in range(TI):
                        last = nc.tensor.matmul(
                            bank[2 * ((t - 1) % 2) + gp][:, b * D:(b + 1) * D],
                            vb[:, (t - 1) * TI + b, gp * P:(gp + 1) * P],
                            pT[:, t % 2, b * D:(b + 1) * D], start=True, stop=True)
                last.then_inc(o_psum, 1)

            def attend_out(t):
                if t == 0:
                    pe.wait_ge(wo_summed, 1)
                    pe.wait_ge(vT_ready, 1)
                    pe.wait_ge(wm_ready, 1)
                    for gp in range(2):
                        last = nc.tensor.matmul(bank[7][0:1, 0:C], vT[:, gp:gp + 1], wo_sum[:, gp, :],
                                                start=gp == 0, stop=gp == 1)
                else:
                    pe.wait_ge(oT_ready, t)
                    pe.wait_ge(h1_ready, t)
                    for k in range(2 * R):
                        last = nc.tensor.matmul(bank[7][:, 0:C], oT[:, t % 2, k // R, k % R, :],
                                                wo_sb[:, k // R, k % R, :],
                                                start=k == 0, stop=k == 2 * R - 1)
                last.then_inc(a_psum, 1)

            def transpose_xq(t):
                pe.wait_ge(xq_ready, t + 1)
                if t == 0:
                    pe.wait_ge(s_read, 4)
                else:
                    pe.wait_ge(xqT_ready, t)
                n = rows(t)
                for c in range(CC):
                    last = nc.tensor.transpose(bankb[4][:, c * P:c * P + n],
                                               xq[0:n, t % 2, c * P:(c + 1) * P], eyeb[0:n, 0:n])
                last.then_inc(xqT_psum, 1)

            def gate_up(t):
                pe.wait_ge(xqT_ready, t + 1)
                for half in range(2):
                    u = 2 * t + half
                    if u < 2:
                        pe.wait_ge(oT_ready, 3 + u)
                        pe.wait_ge(tern_ready, 4)
                    else:
                        pe.wait_ge(g2_ready, u - 1)
                    for i, name in enumerate(("gate", "up")):
                        for c in range(CC):
                            col = c * INNER + half * 512
                            last = nc.tensor.matmul(bank[2 * (u % 2) + i][0:rows(t), :],
                                                    xqT[:, t % 2, c, 0:rows(t)],
                                                    tern[name][:, col:col + 512],
                                                    start=c == 0, stop=c == CC - 1)
                    last.then_inc(gu_psum, 1)

            def transpose_g2(t):
                pe.wait_ge(g2q_ready, t + 1)
                if t == 0:
                    pe.wait_ge(s_read, 4)
                else:
                    pe.wait_ge(g2T_ready, t)
                n = rows(t)
                for c in range(IC):
                    last = nc.tensor.transpose(bankb[5][:, c * P:c * P + n],
                                               g2q[0:n, t % 2, c * P:(c + 1) * P], eyeb[0:n, 0:n])
                last.then_inc(g2T_psum, 1)

            def down(t):
                pe.wait_ge(g2T_ready, t + 1)
                if t == 0:
                    pe.wait_ge(pT_ready, 4)
                    pe.wait_ge(tern_ready, 6)
                else:
                    pe.wait_ge(out_ready, t)
                for c in range(IC):
                    last = nc.tensor.matmul(bank[6][0:rows(t), 0:C], g2T[:, t % 2, c, 0:rows(t)],
                                            tern["down"][:, c * C:(c + 1) * C],
                                            start=c == 0, stop=c == IC - 1)
                last.then_inc(d_psum, 1)

            pe.wait_ge(ld_eyef, 16)
            transpose_y(0)
            for c in range(FC - 2):
                pe.wait_ge(ld_x[c], 32)
                for t in PATCH:
                    nc.tensor.matmul(bank[t - 1][:, 0:C], x_sb[:, c, tcols(t)], wtok_sb[:, c, :],
                                     start=c == 0, stop=False)
            for t in PATCH:
                for c in range(FC - 2, FC):
                    if t == 1:
                        pe.wait_ge(ld_x[c], 32)
                    last = nc.tensor.matmul(bank[t - 1][:, 0:C], x_sb[:, c, tcols(t)],
                                            wtok_sb[:, c, :], start=False, stop=c == FC - 1)
                last.then_inc(embedded, 1)
            pe.wait_ge(ld_wv, 16)
            values(0)
            transpose_y(1)
            transpose_y(2)
            values(1)
            values(2)
            pe.wait_ge(ld_wk, 16)
            project(0)
            pe.wait_ge(v_ready, 2)
            for j in range(2):
                for c in range(CC):
                    last = nc.tensor.matmul(bank[7][:, j:j + 1], wk_sb[:, c, j, :],
                                            yT[:, c, TOK:TOK + 1], start=c == 0, stop=c == CC - 1)
            last.then_inc(kc_psum, 1)
            transpose_y(3)
            transpose_y(4)
            pe.wait_ge(ld_wq[0], 16)
            project(1)
            pe.wait_ge(kc_copied, 1)
            values(3)
            values(4)
            project(2)
            pe.wait_ge(v_ready, 4)
            for gp in range(2):
                last = nc.tensor.transpose(bank[7][:, gp:gp + 1], v_sb[0:1, 0, gp * P:(gp + 1) * P],
                                           eyef[0:1, 0:1])
            last.then_inc(vT_psum, 1)
            pe.wait_ge(ld_wq[1], 16)
            for s in range(3, 8):
                project(s)
            scores(1)
            project(8)
            scores(2)
            project(9)
            pe.wait_ge(abs_done, 3)
            pe.wait_ge(const_ready, 2)
            pe.wait_ge(vT_ready, 1)
            nc.tensor.matmul(bank[7][:, 0:3], ones[:, :], asum[:, 0:3], start=True, stop=True)\
                .then_inc(tot_psum, 1)
            transpose_probs(1)
            mix(1)
            scores(3)
            attend_out(0)
            transpose_probs(2)
            mix(2)
            pe.wait_ge(ld_wo, 16)
            attend_out(1)
            scores(4)
            transpose_probs(3)
            mix(3)
            attend_out(2)
            transpose_probs(4)
            mix(4)
            pe.wait_ge(const_ready, 3)
            attend_out(3)
            transpose_xq(0)
            gate_up(0)
            attend_out(4)
            transpose_xq(1)
            gate_up(1)
            transpose_g2(0)
            down(0)
            for t in range(2, TILES + 1):
                transpose_xq(t)
                gate_up(t)
                transpose_g2(t - 1)
                down(t - 1)
            transpose_g2(TILES)
            down(TILES)

        @block.vector
        def _(dve):
            links = [0]

            def link(ins):
                links[0] += 1
                ins.then_inc(dve_link, 1)
                dve.wait_ge(dve_link, links[0])

            def norm1(t):
                n = rows(t)
                st = stats[0:n, t, 0, :]
                link(nc.vector.bn_stats(st[:, 0:6], h_sb[0:n, t, :]))
                link(nc.vector.bn_aggr(st[:, 6:8], st[:, 0:6]))
                nc.vector.tensor_scalar(rstd[0:n, t, 0, 0:1], st[:, 7:8], EPS, None, ALU.add)\
                    .then_inc(var_ready, 1)
                dve.wait_ge(rstd_ready, t + 1)
                if t >= 2:
                    dve.wait_ge(yT_psum, t - 1)
                nc.vector.tensor_scalar(y_sb[0:n, t % 2, :], h_sb[0:n, t, :], st[:, 6:7],
                                        rstd[0:n, t, 0, 1:2], ALU.subtract, ALU.mult)\
                    .then_inc(y_ready, 1)

            def rotate(s):
                dve.wait_ge(proj_psum, s + 1)
                if s >= 2:
                    dve.wait_ge(roped, s - 1)
                x = bank[s % 4][:, :].rearrange("p (a n) -> p a n", n=N)
                for dst, tab in ((rc, cos_sb), (rs, sin_sb)):
                    last = nc.vector.tensor_tensor(
                        dst[:, s % 2, :, :].rearrange("p j (b n) -> p (j b) n", n=N), x,
                        tab[:, :].unsqueeze(1).broadcast_to([P, 2 * HALF // N, N]), ALU.mult)
                last.then_inc(proj_read, 1)

            def mask_scores(t):
                dve.wait_ge(s_psum, t)
                if t >= 3:
                    dve.wait_ge(exp_done, t - 2)
                nc.vector.tensor_tensor(
                    sc[:, t % 2, :].rearrange("p (a k) -> p a k", k=S),
                    bank[4 + t % 2][:, 0:PAIRS * GK].rearrange("p (a k) -> p a k", k=S),
                    mask_sb[:, :].unsqueeze(1).broadcast_to([P, PAIRS * G, S]), ALU.add)\
                    .then_inc(s_read, 1)
                dve.wait_ge(s_read, t)
                nc.vector.tensor_reduce(smax[:, t % 2, :],
                                        sc[:, t % 2, :].rearrange("p (a k) -> p a k", k=S),
                                        AX_X, ALU.max).then_inc(smax_ready, 1)

            def sum_exps(t):
                dve.wait_ge(exp_done, t)
                link(nc.vector.tensor_reduce(ssum[:, t % 2, :],
                                             ex[:, t % 2, :].rearrange("p (a k) -> p a k", k=S),
                                             AX_X, ALU.add))
                if t >= 3:
                    dve.wait_ge(probs_ready, t - 2)
                nc.vector.reciprocal(srec[:, t % 2, :], ssum[:, t % 2, :]).then_inc(srec_ready, 1)

            def norm2(t):
                n = rows(t)
                st = stats[0:n, t, 1, :]
                z = q1[0:n, t, :]
                dve.wait_ge(a_psum, t + 1)
                nc.vector.tensor_tensor(h_sb[0:n, t, :], bank[7][0:n, 0:C], h_sb[0:n, t, :], ALU.add)\
                    .then_inc(h1_ready, 1)
                dve.wait_ge(h1_ready, t + 1)
                link(nc.vector.bn_stats(st[:, 0:6], h_sb[0:n, t, :]))
                link(nc.vector.bn_aggr(st[:, 6:8], st[:, 0:6]))
                nc.vector.tensor_scalar(rstd[0:n, t, 1, 0:1], st[:, 7:8], EPS, None, ALU.add)\
                    .then_inc(var2_ready, 1)
                link(nc.vector.tensor_scalar(dx[0:n, t % 2, :], h_sb[0:n, t, :], st[:, 6:7], None,
                                             ALU.subtract))
                link(nc.vector.tensor_reduce(z[:, 0:1], dx[0:n, t % 2, :], AX_X, ALU.max,
                                             apply_absolute_value=True))
                dve.wait_ge(rstd2_ready, t + 1)
                r = rstd[0:n, t, 1, 1:2]
                link(nc.vector.tensor_scalar(z[:, 1:2], z[:, 0:1], r, 1e-5, ALU.mult, ALU.max))
                link(nc.vector.reciprocal(z[:, 2:3], z[:, 1:2]))
                link(nc.vector.tensor_scalar(z[:, 3:4], z[:, 2:3], QMAX, r, ALU.mult, ALU.mult))
                link(nc.vector.tensor_scalar(xm[0:n, t % 2, :], dx[0:n, t % 2, :], z[:, 3:4], MAGIC,
                                             ALU.mult, ALU.add))
                if t >= 2:
                    dve.wait_ge(xqT_psum, t - 1)
                nc.vector.tensor_scalar(xq[0:n, t % 2, :], xm[0:n, t % 2, :], -MAGIC, None, ALU.add)\
                    .then_inc(xq_ready, 1)
                nc.vector.tensor_scalar(z[:, 4:5], z[:, 1:2], wdq[0:n, 0:1], None, ALU.mult)
                nc.vector.tensor_scalar(z[:, 5:6], z[:, 1:2], wdq[0:n, 1:2], None, ALU.mult)\
                    .then_inc(scale1_ready, 1)

            def gate_product(t):
                n = rows(t)
                for half in range(2):
                    u = 2 * t + half
                    dve.wait_ge(gu_psum, u + 1)
                    dve.wait_ge(sg_ready, u + 1)
                    nc.vector.tensor_tensor(g2[0:n, t % 2, half * 512:(half + 1) * 512],
                                            bank[2 * (u % 2) + 1][0:n, :],
                                            sg[0:n, t % 2, half * 512:(half + 1) * 512], ALU.mult)\
                        .then_inc(g2_ready, 1)

            def quantise_product(t):
                n = rows(t)
                z = q1[0:n, t, :]
                z5 = z[:, 5:6]
                dve.wait_ge(g2_ready, 2 * t + 2)
                dve.wait_ge(scale1_ready, t + 1)
                link(nc.vector.tensor_reduce(z[:, 0:1], g2[0:n, t % 2, :], AX_X, ALU.max,
                                             apply_absolute_value=True))
                link(nc.vector.tensor_scalar(z[:, 6:7], z[:, 0:1], z5, 1e-5, ALU.mult, ALU.max))
                link(nc.vector.reciprocal(z[:, 2:3], z[:, 6:7]))
                link(nc.vector.tensor_scalar(z[:, 3:4], z[:, 2:3], QMAX, z5, ALU.mult, ALU.mult))
                if t >= 1:
                    dve.wait_ge(g2q_ready, t)
                nc.vector.tensor_scalar(g2m[0:n, :], g2[0:n, t % 2, :], z[:, 3:4], MAGIC,
                                        ALU.mult, ALU.add).then_inc(g2m_ready, 1)
                link(nc.vector.tensor_scalar(z[:, 7:8], z[:, 6:7], wdq[0:n, 2:3], None, ALU.mult))

            def finish(t):
                n = rows(t)
                dve.wait_ge(d_psum, t + 1)
                nc.vector.scalar_tensor_tensor(out=o_sb[0:n, t, :], in0=bank[6][0:n, 0:C],
                                               scalar=q1[0:n, t, 7:8], in1=h_sb[0:n, t, :],
                                               op0=ALU.mult, op1=ALU.add).then_inc(out_ready, 1)

            def ternary(i, half):
                name = ("gate", "up", "down")[i]
                cols = slice(half * INNER, (half + 1) * INNER)
                link(nc.vector.tensor_scalar(below[:, cols], raw[name][:, cols], nthr[:, i:i + 1],
                                             None, ALU.is_lt))
                nc.vector.scalar_tensor_tensor(out=tern[name][:, cols], in0=raw[name][:, cols],
                                               scalar=thr[:, i:i + 1], in1=below[:, cols],
                                               op0=ALU.is_gt, op1=ALU.subtract)\
                    .then_inc(tern_ready, 1)

            nc.vector.memset(mhalf[:, :], -0.5).then_inc(const_ready, 1)
            nc.vector.memset(ones[:, :], 1.0).then_inc(const_ready, 1)
            dve.wait_ge(ld_eyef, 16)
            nc.vector.tensor_copy(eyeb[:, :], eyef[:, :]).then_inc(const_ready, 1)
            dve.wait_ge(ld_cls, 16)
            norm1(0)
            nc.vector.memset(vb[:, 0:B // 2, :], 0.0).then_inc(vb_zero, 1)
            dve.wait_ge(ld_pos, 16)
            dve.wait_ge(ld_b, 16)
            link(nc.vector.tensor_tensor(posb[:, :], pos_sb[:, :], b_sb[:, :], ALU.add))
            for t in PATCH:
                dve.wait_ge(embedded, t)
                nc.vector.tensor_tensor(h_sb[:, t, :], bank[t - 1][:, 0:C], posb[:, :], ALU.add)\
                    .then_inc(h_ready, 1)
                dve.wait_ge(h_ready, t)
                norm1(t)
            dve.wait_ge(ld_tab, 48)
            rotate(0)
            dve.wait_ge(kc_psum, 1)
            nc.vector.tensor_copy(kcls[:, :], bank[7][:, 0:2]).then_inc(kc_copied, 1)
            rotate(1)
            dve.wait_ge(kc_copied, 1)
            dve.wait_ge(kb_zero, 1)
            for j in range(2):
                for g in range(G):
                    ps = slice(g * HD, (g + 1) * HD)
                    last = nc.vector.tensor_copy(kb[ps, j, :, g * S],
                                                 kcls[ps, j:j + 1].broadcast_to([HD, B]))
            last.then_inc(kcls_placed, 1)
            rotate(2)
            dve.wait_ge(vT_psum, 1)
            nc.vector.tensor_copy(vT[:, :], bank[7][:, 0:2]).then_inc(vT_ready, 1)
            for s in range(3, 8):
                rotate(s)
            mask_scores(1)
            rotate(8)
            sum_exps(1)
            mask_scores(2)
            rotate(9)
            sum_exps(2)
            dve.wait_ge(tot_psum, 1)
            nc.vector.tensor_scalar(wm[:, :], bank[7][:, 0:3], 1.0 / (C * INNER), 1e-5,
                                    ALU.mult, ALU.max).then_inc(wm_ready, 1)
            dve.wait_ge(wm_ready, 1)
            link(nc.vector.tensor_scalar(thr[:, :], wm[:, :], 0.5, None, ALU.mult))
            link(nc.vector.tensor_scalar(nthr[:, :], wm[:, :], -0.5, None, ALU.mult))
            link(nc.vector.tensor_scalar(wdq[:, :], wm[:, :], 1.0 / QMAX, None, ALU.mult))
            ternary(0, 0)
            mask_scores(3)
            sum_exps(3)
            norm2(0)
            ternary(0, 1)
            norm2(1)
            mask_scores(4)
            sum_exps(4)
            ternary(1, 0)
            ternary(1, 1)
            norm2(2)
            ternary(2, 0)
            ternary(2, 1)
            norm2(3)
            gate_product(0)
            quantise_product(0)
            norm2(4)
            for t in PATCH:
                gate_product(t)
                quantise_product(t)
                finish(t - 1)
            finish(TILES)

        @block.scalar
        def _(act):
            def copy_yT(t):
                act.wait_ge(yT_psum, t + 1)
                nc.scalar.copy(yT[:, :, tcols(t)],
                               bank[4 + t % 2][:, 0:C].rearrange("p (c n) -> p c n", c=CC)[:, :, 0:rows(t)])\
                    .then_inc(yT_ready, 1)

            def copy_v(t):
                act.wait_ge(v_psum, t + 1)
                nc.scalar.copy(v_sb[0:rows(t), t, :], bank[6 + t % 2][0:rows(t), 0:C])\
                    .then_inc(v_ready, 1)

            def exps(t):
                act.wait_ge(shifted, t)
                if t >= 3:
                    act.wait_ge(pT_psum, t - 2)
                nc.scalar.activation(ex[:, t % 2, :], sc[:, t % 2, :], ACT.Exp, scale=SCALE)\
                    .then_inc(exp_done, 1)

            def copy_pT(t):
                act.wait_ge(pT_psum, t)
                if t >= 3:
                    act.wait_ge(o_psum, t - 2)
                nc.scalar.copy(pT[:, t % 2, :], bank[6][0:GK, :]).then_inc(pT_ready, 1)

            def copy_oT(t):
                act.wait_ge(o_psum, t)
                if t >= 3:
                    act.wait_ge(a_psum, t - 1)
                for gp in range(2):
                    last = nc.scalar.copy(
                        oT[:, t % 2, gp, :, :].rearrange("p r (b n) -> p b r n", n=N),
                        bank[2 * ((t - 1) % 2) + gp][:, :].rearrange("p (b r n) -> p b r n", r=R, n=N))
                last.then_inc(oT_ready, 1)

            def copy_xqT(t):
                act.wait_ge(xqT_psum, t + 1)
                if t >= 2:
                    act.wait_ge(gu_psum, 2 * t - 2)
                n = rows(t)
                nc.scalar.copy(xqT[:, t % 2, :, 0:n],
                               bankb[4][:, 0:C].rearrange("p (c n) -> p c n", c=CC)[:, :, 0:n])\
                    .then_inc(xqT_ready, 1)

            def silu(t):
                n = rows(t)
                act.wait_ge(scale1_ready, t + 1)
                for half in range(2):
                    u = 2 * t + half
                    act.wait_ge(gu_psum, u + 1)
                    if u >= 4:
                        act.wait_ge(g2_ready, u - 3)
                    nc.scalar.activation(sg[0:n, t % 2, half * 512:(half + 1) * 512],
                                         bank[2 * (u % 2)][0:n, :], ACT.Silu,
                                         scale=q1[0:n, t, 4:5]).then_inc(sg_ready, 1)

            def copy_g2T(t):
                act.wait_ge(g2T_psum, t + 1)
                if t >= 2:
                    act.wait_ge(d_psum, t - 1)
                n = rows(t)
                nc.scalar.copy(g2T[:, t % 2, :, 0:n],
                               bankb[5].rearrange("p (c n) -> p c n", c=IC)[:, :, 0:n])\
                    .then_inc(g2T_ready, 1)

            copy_yT(0)
            copy_v(0)
            copy_yT(1)
            copy_yT(2)
            copy_v(1)
            copy_v(2)
            copy_yT(3)
            copy_yT(4)
            copy_v(3)
            copy_v(4)
            for i, (name, s) in enumerate((("gate", ld_gate), ("up", ld_up), ("down", ld_down))):
                act.wait_ge(s, 16)
                if i:
                    act.wait_ge(abs_done, i)
                nc.scalar.activation(abs_junk[:, :], raw[name][:, :], ACT.Abs,
                                     accum_out=asum[:, i:i + 1]).then_inc(abs_done, 1)
            exps(1)
            exps(2)
            copy_pT(1)
            copy_oT(1)
            copy_pT(2)
            exps(3)
            copy_oT(2)
            copy_pT(3)
            exps(4)
            copy_oT(3)
            copy_pT(4)
            copy_oT(4)
            copy_xqT(0)
            silu(0)
            copy_xqT(1)
            silu(1)
            copy_g2T(0)
            for t in range(2, TILES + 1):
                copy_xqT(t)
                silu(t)
                copy_g2T(t - 1)
            copy_g2T(TILES)

        @block.gpsimd
        def _(pool):
            def inv_std(t, i, ready, done):
                n = rows(t)
                pool.wait_ge(ready, t + 1)
                nc.gpsimd.tensor_tensor(rstd[0:n, t, i, 1:2], rstd[0:n, t, i, 0:1], mhalf[0:n, :],
                                        ALU.pow).then_inc(done, 1)

            def combine(s):
                half, r = divmod(s, R + 1)
                pool.wait_ge(proj_read, s + 1)
                if s in (1, R + 1, R + 2):
                    pool.wait_ge(roped, s)
                a, b = rc[:, s % 2, :, :], rs[:, s % 2, :, :]
                parts = ((0, a[:, 0, :], b[:, 1, :], ALU.subtract), (1, b[:, 0, :], a[:, 1, :], ALU.add))
                for j, left, right, op in parts:
                    bs = slice(half * B // 2, (half + 1) * B // 2)
                    if r:
                        last = nc.gpsimd.tensor_tensor(
                            qr[:, j, bs, r - 1, :], left.rearrange("p (b n) -> p b n", n=N),
                            right.rearrange("p (b n) -> p b n", n=N), op)
                        continue
                    for g in range(G):
                        ps = slice(g * HD, (g + 1) * HD)
                        last = nc.gpsimd.tensor_tensor(
                            kb[ps, j, bs, g * S + 1:(g + 1) * S],
                            left[ps].rearrange("p (b n) -> p b n", n=N),
                            right[ps].rearrange("p (b n) -> p b n", n=N), op)
                last.then_inc(roped, 1)

            def shift(t):
                pool.wait_ge(smax_ready, t)
                v = sc[:, t % 2, :].rearrange("p (a k) -> p a k", k=S)
                nc.gpsimd.tensor_tensor(v, v, smax[:, t % 2, :].unsqueeze(2)
                                        .broadcast_to([P, PAIRS * G, S]), ALU.subtract)\
                    .then_inc(shifted, 1)

            def normalise(t):
                pool.wait_ge(srec_ready, t)
                v = ex[:, t % 2, :].rearrange("p (a k) -> p a k", k=S)
                nc.gpsimd.tensor_tensor(v, v, srec[:, t % 2, :].unsqueeze(2)
                                        .broadcast_to([P, PAIRS * G, S]), ALU.mult)\
                    .then_inc(probs_ready, 1)

            def round_product(t):
                pool.wait_ge(g2m_ready, t + 1)
                if t >= 2:
                    pool.wait_ge(g2T_psum, t - 1)
                n = rows(t)
                nc.gpsimd.tensor_scalar(g2q[0:n, t % 2, :], g2m[0:n, :], 1.0, -MAGIC,
                                        ALU.mult, ALU.add).then_inc(g2q_ready, 1)

            nc.gpsimd.memset(kb[:, :, :, :], 0.0).then_inc(kb_zero, 1)
            pool.wait_ge(const_ready, 1)
            pool.wait_ge(kb_zero, 1)
            inv_std(0, 0, var_ready, rstd_ready)
            nc.gpsimd.memset(vb[:, B // 2:B, :], 0.0).then_inc(vb_zero, 1)
            for t in PATCH:
                inv_std(t, 0, var_ready, rstd_ready)
            for s in range(6):
                combine(s)
            pool.wait_ge(ld_wo, 16)
            pool.wait_ge(roped, 6)
            for gp in range(2):
                links = 2 * gp
                pool_steps = ((wo_sb[:, gp, 0, :], wo_sb[:, gp, 1, :]),
                              (wo_sum[:, gp, :], wo_sb[:, gp, 2, :]),
                              (wo_sum[:, gp, :], wo_sb[:, gp, 3, :]))
                for i, (a, b) in enumerate(pool_steps):
                    if i:
                        pool.wait_ge(pool_link, links + i)
                    ins = nc.gpsimd.tensor_tensor(wo_sum[:, gp, :], a, b, ALU.add)
                    if i < 2:
                        ins.then_inc(pool_link, 1)
            ins.then_inc(wo_summed, 1)
            combine(6)
            combine(7)
            shift(1)
            combine(8)
            normalise(1)
            shift(2)
            combine(9)
            normalise(2)
            shift(3)
            normalise(3)
            inv_std(0, 1, var2_ready, rstd2_ready)
            inv_std(1, 1, var2_ready, rstd2_ready)
            shift(4)
            normalise(4)
            inv_std(2, 1, var2_ready, rstd2_ready)
            inv_std(3, 1, var2_ready, rstd2_ready)
            round_product(0)
            inv_std(4, 1, var2_ready, rstd2_ready)
            for t in PATCH:
                round_product(t)


def shape_constants():
    import numpy as np
    inv = (1.0 / np.float32(10000.0) ** (np.arange(0, D, 2, dtype=np.float32) / np.float32(D)))
    ang = np.arange(1, S, dtype=np.float32)[None, :] * inv.astype(np.float32)[:, None]
    cos_t = np.tile(np.cos(ang).astype(np.float32), (G, 1))
    sin_t = np.tile(np.sin(ang).astype(np.float32), (G, 1))
    q = np.arange(P)[:, None] % N + 1
    mask_t = np.where(np.arange(S)[None, :] <= q, 0.0, MASKED).astype(np.float32)
    return {"cos_t": cos_t, "sin_t": sin_t, "mask_t": mask_t,
            "eye_f": np.eye(P, dtype=np.float32)}


def kernel(**inputs):
    import numpy as np
    import concourse.bacc as bacc
    from concourse.bass_utils import run_bass_kernel_spmd

    a = {k: np.asarray(v) for k, v in inputs.items()}
    ps = 16
    lay = {
        "xT": a["x"].reshape(B, 3, 4, ps, 4, ps).transpose(1, 3, 5, 0, 2, 4).reshape(FC, P, TOK),
        "w_tok": a["L0_tok_W"].T.reshape(FC, P, C),
        "tok_b": a["L0_tok_b"].reshape(1, C),
        "pos": np.tile(a["L0_tok_pos_emb"], (TI, 1)),
        "cls_tok": a["cls_tok"].reshape(1, C),
        "wq": a["L0_attn_Wq"].reshape(CC, P, G, R, HD, 2).transpose(1, 0, 3, 5, 2, 4)
                             .reshape(P, CC, R, 2, P),
        "wk": a["L0_attn_Wk"].reshape(CC, P, G, HD, 2).transpose(1, 0, 4, 2, 3).reshape(P, CC, 2, P),
        "wv": a["L0_attn_Wv"].reshape(CC, P, C).transpose(1, 0, 2),
        "wo": a["L0_attn_Wo"].reshape(2, 2, R, D, C).transpose(1, 3, 0, 2, 4).reshape(P, 2, R, C),
        "w_gate": a["L0_ffn_w_gate"].T.reshape(CC, P, INNER).transpose(1, 0, 2).reshape(P, 2 * INNER),
        "w_up": a["L0_ffn_w_up"].T.reshape(CC, P, INNER).transpose(1, 0, 2).reshape(P, 2 * INNER),
        "w_down": a["L0_ffn_w_down"].T.reshape(IC, P, C).transpose(1, 0, 2).reshape(P, 2 * INNER),
    }
    lay.update(shape_constants())

    nc = bacc.Bacc("TRN2", target_bir_lowering=False, num_devices=1)
    arrays, args = {}, {}
    for name, v in lay.items():
        v = np.ascontiguousarray(v)
        arrays[f"in_{name}"] = v
        args[name] = nc.dram_tensor(f"in_{name}", v.shape, mybir.dt.from_np(v.dtype),
                                    kind="ExternalInput").ap()
    out = nc.dram_tensor("out_0", (B, S, C), F32, kind="ExternalOutput").ap()
    build(nc, out=out, **args)
    r = run_bass_kernel_spmd(nc, [arrays], core_ids=[0])
    return r.results[0]["out_0"]
```

```python
from contextlib import ExitStack

import concourse.bass as bass
from concourse import mybir

ALU = mybir.AluOpType
ACT = mybir.ActivationFunctionType
F32 = mybir.dt.float32
BF16 = mybir.dt.bfloat16
AX_X = mybir.AxisListType.X

P = 128
B = 32
N = 16
S = N + 1
C = 256
CC = C // P
IN_FEAT = 768
FC = IN_FEAT // P
G, R, D = 4, 4, 64
HD = D // 2
INNER = 1024
IC = INNER // P
TOK = B * N
TILES = TOK // P
TI = P // N
PAIRS = TI // 2
HALF = TOK // 2
GK = G * S
EPS = 1e-5
MASKED = -1e30
MAGIC = 1.5 * 2.0 ** 23
QMAX = 127.0
SCALE = float(D) ** -0.5
WARM = 9


def build(nc, xT, w_tok, tok_b, pos, cls_tok, wq, wk, wv, wo, w_gate, w_up, w_down,
          cos_t, sin_t, mask_t, eye_f, out):
    with ExitStack() as ctx:
        def sb(name, shape, dt=F32):
            return ctx.enter_context(nc.sbuf_tensor(name, shape, dt))

        def sem(name):
            return ctx.enter_context(nc.semaphore(name))

        x_sb = sb("x_sb", [P, FC, TOK])
        wtok_sb = sb("wtok_sb", [P, FC, C])
        b_sb = sb("b_sb", [P, C])
        pos_sb = sb("pos_sb", [P, C])
        posb = sb("posb", [P, C])
        wq_sb = sb("wq_sb", [P, CC, R, 2, P])
        wk_sb = sb("wk_sb", [P, CC, 2, P])
        wv_sb = sb("wv_sb", [P, CC, C])
        wo_sb = sb("wo_sb", [P, 2, R, C])
        wo_sum = sb("wo_sum", [P, 2, C])
        raw = {n: sb(f"raw_{n}", [P, 2 * INNER]) for n in ("gate", "up", "down")}
        tern = {n: sb(f"tern_{n}", [P, 2 * INNER], BF16) for n in ("gate", "up", "down")}
        cos_sb = sb("cos_sb", [P, N])
        sin_sb = sb("sin_sb", [P, N])
        mask_sb = sb("mask_sb", [P, S])
        eyef = sb("eyef", [P, P])
        eyeb = sb("eyeb", [P, P], BF16)
        ones = sb("ones", [P, P])
        mhalf = sb("mhalf", [P, 1])
        magic = sb("magic", [P, 2])
        h_sb = sb("h_sb", [P, TILES + 1, C])
        y_sb = sb("y_sb", [P, 2, C])
        yT = sb("yT", [P, CC, TOK + 1])
        stats = sb("stats", [P, TILES + 1, 2, 8])
        rstd = sb("rstd", [P, TILES + 1, 2, 2])
        rc = sb("rc", [P, 2, 2, HALF])
        rs = sb("rs", [P, 2, 2, HALF])
        kr = sb("kr", [P, 2, HALF])
        qr = sb("qr", [P, 2, B, R, N])
        kb = sb("kb", [P, 2, B, GK])
        kcls = sb("kcls", [P, 2])
        v_sb = sb("v_sb", [P, TILES + 1, C])
        vb = sb("vb", [GK, B, C])
        vT = sb("vT", [P, 2])
        sc = sb("sc", [P, TILES, PAIRS * GK])
        ex = sb("ex", [P, TILES, PAIRS * GK])
        smax = sb("smax", [P, TILES, PAIRS * G])
        ssum = sb("ssum", [P, TILES, PAIRS * G])
        srec = sb("srec", [P, TILES, PAIRS * G])
        pT = sb("pT", [GK, 2, PAIRS * P])
        oT = sb("oT", [P, 2, 2, R, P])
        asum = sb("asum", [P, 4])
        wm = sb("wm", [P, 3])
        wscale = sb("wscale", [P, 3])
        wdq = sb("wdq", [P, 3])
        q1 = sb("q1", [P, TILES + 1, 8])
        dx = sb("dx", [P, 2, C])
        xm = sb("xm", [P, 2, C])
        xq = sb("xq", [P, 2, C], BF16)
        xqT = sb("xqT", [P, 2, CC, P], BF16)
        sg = x_sb[:, 0:4, :].rearrange("p (a b) n -> p a (b n)", a=2)
        g2 = (x_sb[:, 4:6, :].rearrange("p a n -> p (a n)"),
              wtok_sb[:, 0:4, :].rearrange("p a n -> p (a n)"))
        g2m = rc[:, :, :, :].rearrange("p a j n -> p (a j n)")
        g2q = sb("g2q", [P, 2, INNER], BF16)
        g2T = sb("g2T", [P, 2, IC, P], BF16)
        o_sb = h_sb
        v_dram = nc.dram_tensor("v_scratch", [TOK + 1, C], F32, kind="Internal").ap()

        bank = [ctx.enter_context(nc.psum_tensor(f"bank{i}", [P, 512], F32)) for i in range(8)]
        bankb = [b[:, :].bitcast(BF16) for b in bank]

        ld_cls, ld_pos, ld_b, ld_eyef, ld_tab = (sem(n) for n in (
            "ld_cls", "ld_pos", "ld_b", "ld_eyef", "ld_tab"))
        ld_x = [sem(f"ld_x{c}") for c in range(FC)]
        ld_wk, ld_wv, ld_wo, ld_gate, ld_up, ld_down = (sem(n) for n in (
            "ld_wk", "ld_wv", "ld_wo", "ld_gate", "ld_up", "ld_down"))
        ld_wq = [sem(f"ld_wq{c}") for c in range(2)]
        v_stored = sem("v_stored")
        vb_loaded = [sem(f"vb_loaded{h}") for h in range(3)]
        stored = sem("stored")
        const_ready, kb_zero, vb_zero = sem("const_ready"), sem("kb_zero"), sem("vb_zero")
        ones_ready = sem("ones_ready")
        embedded, posb_ready, h_ready = sem("embedded"), sem("posb_ready"), sem("h_ready")
        dve_link, pool_link, act_link = sem("dve_link"), sem("pool_link"), sem("act_link")
        var_ready, rstd_ready, y_ready = sem("var_ready"), sem("rstd_ready"), sem("y_ready")
        yT_psum, yT_ready = sem("yT_psum"), sem("yT_ready")
        v_psum, v_ready = sem("v_psum"), sem("v_ready")
        kc_psum, kc_copied = sem("kc_psum"), sem("kc_copied")
        vT_psum, vT_ready = sem("vT_psum"), sem("vT_ready")
        proj_psum, proj_read, roped = sem("proj_psum"), sem("proj_read"), sem("roped")
        kcls_placed, k_rotated, k_placed = sem("kcls_placed"), sem("k_rotated"), sem("k_placed")
        abs_done, tot_psum, wm_ready, tern_ready = (sem(n) for n in (
            "abs_done", "tot_psum", "wm_ready", "tern_ready"))
        wscale_ready, lifted, rounded = sem("wscale_ready"), sem("lifted"), sem("rounded")
        wo_summed = sem("wo_summed")
        s_psum, s_read, smax_ready, shifted, exp_done = (sem(n) for n in (
            "s_psum", "s_read", "smax_ready", "shifted", "exp_done"))
        srec_ready, probs_ready, pT_psum, pT_ready = (sem(n) for n in (
            "srec_ready", "probs_ready", "pT_psum", "pT_ready"))
        o_psum, oT_ready, a_psum, h1_ready = (sem(n) for n in (
            "o_psum", "oT_ready", "a_psum", "h1_ready"))
        var2_ready, rstd2_ready, xq_ready, xqT_psum, xqT_ready = (sem(n) for n in (
            "var2_ready", "rstd2_ready", "xq_ready", "xqT_psum", "xqT_ready"))
        gu_psum, sg_ready, g2_ready, g2m_ready, g2q_ready, g2T_psum, g2T_ready = (sem(n) for n in (
            "gu_psum", "sg_ready", "g2_ready", "g2m_ready", "g2q_ready", "g2T_psum", "g2T_ready"))
        scale1_ready, scale2_ready = sem("scale1_ready"), sem("scale2_ready")
        d_psum, out_ready = sem("d_psum"), sem("out_ready")

        block = ctx.enter_context(nc.Block())

        def rows(t):
            return 1 if t == 0 else P

        def tcols(t):
            return slice(TOK, TOK + 1) if t == 0 else slice((t - 1) * P, t * P)

        def combined(s):
            return s - s // (R + 1)

        ALL = range(TILES + 1)
        PATCH = range(1, TILES + 1)

        @block.sync
        def _(sp):
            for c in range(FC):
                sp.dma_start(x_sb[:, c, :], xT[c]).then_inc(ld_x[c], 16)
                if c:
                    sp.dma_start(wtok_sb[:, c, :], w_tok[c]).then_inc(ld_x[c], 16)
            sp.dma_start(pos_sb[:, :], pos).then_inc(ld_pos, 16)
            sp.dma_start(wv_sb[:, :, :], wv).then_inc(ld_wv, 16)
            sp.dma_start(wk_sb[:, :, :, :], wk).then_inc(ld_wk, 16)
            sp.dma_start(cos_sb[:, :], cos_t).then_inc(ld_tab, 16)
            sp.dma_start(sin_sb[:, :], sin_t).then_inc(ld_tab, 16)
            sp.dma_start(mask_sb[:, :], mask_t).then_inc(ld_tab, 16)
            for c in range(2):
                sp.dma_start(wq_sb[:, :, 2 * c:2 * c + 2, :, :], wq[:, :, 2 * c:2 * c + 2, :, :])\
                    .then_inc(ld_wq[c], 16)
            sp.dma_start(wo_sb[:, :, :, :], wo).then_inc(ld_wo, 16)
            sp.dma_start(raw["gate"][:, :], w_gate).then_inc(ld_gate, 16)
            sp.dma_start(raw["up"][:, :], w_up).then_inc(ld_up, 16)
            sp.dma_start(raw["down"][:, :], w_down).then_inc(ld_down, 16)

            for t in ALL:
                sp.wait_ge(v_ready, t + 1)
                dst = v_dram[TOK:TOK + 1, :] if t == 0 else v_dram[(t - 1) * P:t * P, :]
                sp.dma_start(dst, v_sb[0:rows(t), t, :]).then_inc(v_stored, 16)
            sp.wait_ge(vb_zero, 2)
            sp.wait_ge(v_stored, 16 * (TILES + 1))
            vg = v_dram[0:TOK, :].rearrange("(b n) (g d) -> g n b d", n=N, g=G)
            for g in range(G):
                sp.dma_start(vb[g * S:g * S + 1, :, g * D:(g + 1) * D],
                             v_dram[TOK:TOK + 1, g * D:(g + 1) * D].unsqueeze(1)
                             .broadcast_to([1, B, D])).then_inc(vb_loaded[0], 16)
            for half in range(2):
                bs = slice(half * B // 2, (half + 1) * B // 2)
                for g in range(G):
                    sp.dma_start(vb[g * S + 1:(g + 1) * S, bs, g * D:(g + 1) * D],
                                 vg[g, :, bs, :]).then_inc(vb_loaded[1 + half], 16)
            for t in ALL:
                sp.wait_ge(out_ready, t + 1)
                if t == 0:
                    sp.dma_start(out[:, 0:1, :].rearrange("b s c -> s b c"),
                                 o_sb[0:1, 0, :].unsqueeze(1).broadcast_to([1, B, C]))\
                        .then_inc(stored, 16)
                else:
                    sp.dma_start(out[(t - 1) * TI:t * TI, 1:S, :], o_sb[:, t, :]).then_inc(stored, 16)
            sp.wait_ge(stored, 16 * (TILES + 1))

        @block.tensor
        def _(pe):
            def transpose_y(t):
                pe.wait_ge(y_ready, t + 1)
                if t >= 2:
                    pe.wait_ge(yT_ready, t - 1)
                n = rows(t)
                for c in range(CC):
                    last = nc.tensor.transpose(bank[4 + t % 2][:, c * P:c * P + n],
                                               y_sb[0:n, t % 2, c * P:(c + 1) * P], eyef[0:n, 0:n])
                last.then_inc(yT_psum, 1)

            def values(t):
                pe.wait_ge(yT_ready, t + 1)
                if t >= 2:
                    pe.wait_ge(v_ready, t - 1)
                if t == 3:
                    pe.wait_ge(kc_copied, 1)
                for c in range(CC):
                    last = nc.tensor.matmul(bank[6 + t % 2][0:rows(t), 0:C], yT[:, c, tcols(t)],
                                            wv_sb[:, c, :], start=c == 0, stop=c == CC - 1)
                last.then_inc(v_psum, 1)

            def project(s):
                half, r = divmod(s, R + 1)
                w = wk_sb[:, :, :, :] if r == 0 else wq_sb[:, :, r - 1, :, :]
                if s < 4:
                    pe.wait_ge(h_ready, s + 1)
                else:
                    pe.wait_ge(proj_read, s - 3)
                pe.wait_ge(yT_ready, 3 + 2 * half)
                for j in range(2):
                    for c in range(CC):
                        last = nc.tensor.matmul(bank[s % 4][:, j * HALF:(j + 1) * HALF], w[:, c, j, :],
                                                yT[:, c, half * HALF:(half + 1) * HALF],
                                                start=c == 0, stop=c == CC - 1)
                last.then_inc(proj_psum, 1)

            def scores(t):
                half = (t - 1) // 2
                pe.wait_ge(k_placed, half + 1)
                pe.wait_ge(roped, R * (half + 1))
                if t == 1:
                    pe.wait_ge(kcls_placed, 1)
                if t <= 2:
                    pe.wait_ge(yT_ready, 3 + t)
                else:
                    pe.wait_ge(s_read, t - 2)
                for b in range(TI):
                    img, row = (t - 1) * TI + b, b % 2 * D
                    for j in range(2):
                        last = nc.tensor.matmul(
                            bank[4 + t % 2][row:row + D, b // 2 * GK:(b // 2 + 1) * GK],
                            qr[:, j, img, :, :].rearrange("p r n -> p (r n)"), kb[:, j, img, :],
                            start=j == 0, stop=j == 1)
                last.then_inc(s_psum, 1)

            def transpose_probs(t, free):
                pe.wait_ge(*free)
                pe.wait_ge(probs_ready, t)
                for pr in range(PAIRS):
                    last = nc.tensor.transpose(bank[6][0:GK, pr * P:(pr + 1) * P],
                                               ex[:, t - 1, pr * GK:(pr + 1) * GK], eyef[:, :])
                last.then_inc(pT_psum, 1)

            def mix(t):
                pe.wait_ge(pT_ready, t)
                if t == 1:
                    pe.wait_ge(vb_loaded[0], 16 * G)
                if t % 2:
                    pe.wait_ge(vb_loaded[1 + t // 2], 16 * G)
                if t == 1:
                    pe.wait_ge(proj_read, 10)
                else:
                    pe.wait_ge(oT_ready, 2 * t - 2)
                if t >= 2:
                    pe.wait_ge(xqT_ready, t - 1)
                for gp in range(2):
                    for b in range(TI):
                        last = nc.tensor.matmul(
                            bank[gp][:, b * D:(b + 1) * D],
                            vb[:, (t - 1) * TI + b, gp * P:(gp + 1) * P],
                            pT[:, t % 2, b * D:(b + 1) * D], start=True, stop=True)
                    last.then_inc(o_psum, 1)

            def attend_out(t, free):
                pe.wait_ge(*free)
                if t == 0:
                    pe.wait_ge(wo_summed, 1)
                    pe.wait_ge(vT_ready, 1)
                    for gp in range(2):
                        last = nc.tensor.matmul(bank[7][0:1, 0:C], vT[:, gp:gp + 1], wo_sum[:, gp, :],
                                                start=gp == 0, stop=gp == 1)
                else:
                    for k in range(2 * R):
                        if k % R == 0:
                            pe.wait_ge(oT_ready, 2 * t - 1 + k // R)
                        last = nc.tensor.matmul(bank[7][:, 0:C], oT[:, t % 2, k // R, k % R, :],
                                                wo_sb[:, k // R, k % R, :],
                                                start=k == 0, stop=k == 2 * R - 1)
                last.then_inc(a_psum, 1)

            def transpose_xq(t):
                pe.wait_ge(oT_ready, 2 * min(t + 1, TILES))
                if t == TILES:
                    pe.wait_ge(xqT_ready, t)
                pe.wait_ge(xq_ready, t + 1)
                n = rows(t)
                for c in range(CC):
                    last = nc.tensor.transpose(bankb[0][:, c * P:c * P + n],
                                               xq[0:n, t % 2, c * P:(c + 1) * P], eyeb[0:n, 0:n])
                last.then_inc(xqT_psum, 1)

            def gate_up(t):
                pe.wait_ge(xqT_ready, t + 1)
                if t == 0:
                    pe.wait_ge(proj_read, 8)
                    pe.wait_ge(tern_ready, 4)
                for half in range(2):
                    if t:
                        pe.wait_ge(g2_ready, 2 * t + half - 1)
                    elif half:
                        pe.wait_ge(s_read, TILES)
                    for i, name in enumerate(("gate", "up")):
                        for c in range(CC):
                            col = c * INNER + half * 512
                            last = nc.tensor.matmul(bank[2 + 2 * half + i][0:rows(t), :],
                                                    xqT[:, t % 2, c, 0:rows(t)],
                                                    tern[name][:, col:col + 512],
                                                    start=c == 0, stop=c == CC - 1)
                    last.then_inc(gu_psum, 1)

            def transpose_g2(t, free):
                pe.wait_ge(*free)
                n = rows(t)
                for half in range(2):
                    pe.wait_ge(g2q_ready, 2 * t + half + 1)
                    for c in range(half * IC // 2, (half + 1) * IC // 2):
                        last = nc.tensor.transpose(bankb[6][:, c * P:c * P + n],
                                                   g2q[0:n, t % 2, c * P:(c + 1) * P], eyeb[0:n, 0:n])
                last.then_inc(g2T_psum, 1)

            def down(t, free):
                pe.wait_ge(*free)
                if t == 0:
                    pe.wait_ge(tern_ready, 6)
                for c in range(IC):
                    if c % (IC // 2) == 0:
                        pe.wait_ge(g2T_ready, 2 * t + 1 + c // (IC // 2))
                    last = nc.tensor.matmul(bank[7][0:rows(t), 0:C], g2T[:, t % 2, c, 0:rows(t)],
                                            tern["down"][:, c * C:(c + 1) * C],
                                            start=c == 0, stop=c == IC - 1)
                last.then_inc(d_psum, 1)

            pe.wait_ge(ones_ready, 1)
            for _ in range(WARM):
                nc.tensor.matmul(bank[7][:, 0:P], ones[:, :], ones[:, :], start=True, stop=True)
            pe.wait_ge(ld_eyef, 16)
            transpose_y(0)
            for c in range(FC - 2):
                pe.wait_ge(ld_x[c], 32)
                for t in PATCH:
                    nc.tensor.matmul(bank[t - 1][:, 0:C], x_sb[:, c, tcols(t)], wtok_sb[:, c, :],
                                     start=c == 0, stop=False)
            for t in PATCH:
                for c in range(FC - 2, FC):
                    if t == 1:
                        pe.wait_ge(ld_x[c], 32)
                    last = nc.tensor.matmul(bank[t - 1][:, 0:C], x_sb[:, c, tcols(t)],
                                            wtok_sb[:, c, :], start=False, stop=c == FC - 1)
                last.then_inc(embedded, 1)
            pe.wait_ge(ld_wv, 16)
            values(0)
            transpose_y(1)
            transpose_y(2)
            pe.wait_ge(ld_wk, 16)
            project(0)
            values(1)
            values(2)
            pe.wait_ge(v_ready, 2)
            for j in range(2):
                for c in range(CC):
                    last = nc.tensor.matmul(bank[7][:, j:j + 1], wk_sb[:, c, j, :],
                                            yT[:, c, TOK:TOK + 1], start=c == 0, stop=c == CC - 1)
            last.then_inc(kc_psum, 1)
            transpose_y(3)
            pe.wait_ge(ld_wq[0], 16)
            project(1)
            transpose_y(4)
            project(2)
            values(3)
            values(4)
            pe.wait_ge(v_ready, 4)
            for gp in range(2):
                last = nc.tensor.transpose(bank[7][:, gp:gp + 1], v_sb[0:1, 0, gp * P:(gp + 1) * P],
                                           eyef[0:1, 0:1])
            last.then_inc(vT_psum, 1)
            pe.wait_ge(ld_wq[1], 16)
            project(3)
            project(4)
            project(5)
            project(6)
            pe.wait_ge(abs_done, 3)
            pe.wait_ge(vT_ready, 1)
            nc.tensor.matmul(bank[7][:, 0:3], ones[:, :], asum[:, 0:3], start=True, stop=True)\
                .then_inc(tot_psum, 1)
            scores(1)
            project(7)
            scores(2)
            project(8)
            project(9)
            transpose_probs(1, (v_ready, TILES + 1))
            scores(3)
            mix(1)
            attend_out(0, (wm_ready, 1))
            scores(4)
            pe.wait_ge(ld_wo, 16)
            pe.wait_ge(const_ready, 4)
            attend_out(1, (h1_ready, 1))
            transpose_xq(0)
            gate_up(0)
            transpose_probs(2, (pT_ready, 1))
            mix(2)
            attend_out(2, (h1_ready, 2))
            transpose_xq(1)
            transpose_g2(0, (pT_ready, 2))
            gate_up(1)
            transpose_probs(3, (g2T_ready, 2))
            down(0, (h1_ready, 3))
            mix(3)
            attend_out(3, (out_ready, 1))
            transpose_xq(2)
            transpose_g2(1, (pT_ready, 3))
            gate_up(2)
            transpose_probs(4, (g2T_ready, 4))
            down(1, (h1_ready, 4))
            mix(4)
            attend_out(4, (out_ready, 2))
            transpose_xq(3)
            transpose_g2(2, (pT_ready, 4))
            gate_up(3)
            down(2, (h1_ready, 5))
            transpose_xq(4)
            transpose_g2(3, (g2T_ready, 6))
            gate_up(4)
            down(3, (out_ready, 3))
            transpose_g2(4, (g2T_ready, 8))
            down(4, (out_ready, 4))

        @block.vector
        def _(dve):
            links = [0]

            def link(ins):
                links[0] += 1
                ins.then_inc(dve_link, 1)
                dve.wait_ge(dve_link, links[0])

            def variance(t):
                n = rows(t)
                st = stats[0:n, t, 0, :]
                if t:
                    dve.wait_ge(embedded, t)
                    nc.vector.tensor_tensor(h_sb[:, t, :], bank[t - 1][:, 0:C], posb[:, :], ALU.add)\
                        .then_inc(h_ready, 1)
                    dve.wait_ge(h_ready, t)
                link(nc.vector.bn_stats(st[:, 0:6], h_sb[0:n, t, :]))
                link(nc.vector.bn_aggr(st[:, 6:8], st[:, 0:6]))
                nc.vector.tensor_scalar(rstd[0:n, t, 0, 0:1], st[:, 7:8], EPS, None, ALU.add)\
                    .then_inc(var_ready, 1)

            def norm1(t):
                n = rows(t)
                dve.wait_ge(rstd_ready, t + 1)
                if t >= 2:
                    dve.wait_ge(yT_psum, t - 1)
                nc.vector.tensor_scalar(y_sb[0:n, t % 2, :], h_sb[0:n, t, :], stats[0:n, t, 0, 6:7],
                                        rstd[0:n, t, 0, 1:2], ALU.subtract, ALU.mult)\
                    .then_inc(y_ready, 1)

            def rotate(s):
                dve.wait_ge(proj_psum, s + 1)
                if s >= 2 and combined(s - 2):
                    dve.wait_ge(roped, combined(s - 2))
                x = bank[s % 4][:, :].rearrange("p (a n) -> p a n", n=N)
                for dst, tab in ((rc, cos_sb), (rs, sin_sb)):
                    last = nc.vector.tensor_tensor(
                        dst[:, s % 2, :, :].rearrange("p j (b n) -> p (j b) n", n=N), x,
                        tab[:, :].unsqueeze(1).broadcast_to([P, 2 * HALF // N, N]), ALU.mult)
                last.then_inc(proj_read, 1)
                if s % (R + 1):
                    return
                half = s // (R + 1)
                dve.wait_ge(proj_read, s + 1)
                if half:
                    dve.wait_ge(k_placed, half)
                nc.vector.tensor_tensor(kr[:, 0, :], rc[:, s % 2, 0, :], rs[:, s % 2, 1, :],
                                        ALU.subtract)
                nc.vector.tensor_tensor(kr[:, 1, :], rs[:, s % 2, 0, :], rc[:, s % 2, 1, :],
                                        ALU.add).then_inc(k_rotated, 1)

            def mask_scores(t):
                dve.wait_ge(s_psum, t)
                v = sc[:, t - 1, :].rearrange("p (a k) -> p a k", k=S)
                nc.vector.tensor_tensor(
                    v, bank[4 + t % 2][:, 0:PAIRS * GK].rearrange("p (a k) -> p a k", k=S),
                    mask_sb[:, :].unsqueeze(1).broadcast_to([P, PAIRS * G, S]), ALU.add)\
                    .then_inc(s_read, 1)
                dve.wait_ge(s_read, t)
                nc.vector.tensor_reduce(smax[:, t - 1, :], v, AX_X, ALU.max).then_inc(smax_ready, 1)

            def sum_exps(t):
                dve.wait_ge(exp_done, t)
                link(nc.vector.tensor_reduce(ssum[:, t - 1, :],
                                             ex[:, t - 1, :].rearrange("p (a k) -> p a k", k=S),
                                             AX_X, ALU.add))
                nc.vector.reciprocal(srec[:, t - 1, :], ssum[:, t - 1, :]).then_inc(srec_ready, 1)

            def norm2(t):
                n = rows(t)
                st = stats[0:n, t, 1, :]
                z = q1[0:n, t, :]
                dve.wait_ge(a_psum, t + 1)
                nc.vector.tensor_tensor(h_sb[0:n, t, :], bank[7][0:n, 0:C], h_sb[0:n, t, :], ALU.add)\
                    .then_inc(h1_ready, 1)
                dve.wait_ge(h1_ready, t + 1)
                link(nc.vector.bn_stats(st[:, 0:6], h_sb[0:n, t, :]))
                link(nc.vector.bn_aggr(st[:, 6:8], st[:, 0:6]))
                nc.vector.tensor_scalar(rstd[0:n, t, 1, 0:1], st[:, 7:8], EPS, None, ALU.add)\
                    .then_inc(var2_ready, 1)
                link(nc.vector.tensor_scalar(dx[0:n, t % 2, :], h_sb[0:n, t, :], st[:, 6:7], None,
                                             ALU.subtract))
                link(nc.vector.tensor_reduce(z[:, 0:1], dx[0:n, t % 2, :], AX_X, ALU.max,
                                             apply_absolute_value=True))
                dve.wait_ge(rstd2_ready, t + 1)
                r = rstd[0:n, t, 1, 1:2]
                link(nc.vector.tensor_scalar(z[:, 1:2], z[:, 0:1], r, 1e-5, ALU.mult, ALU.max))
                link(nc.vector.reciprocal(z[:, 2:3], z[:, 1:2]))
                link(nc.vector.tensor_scalar(z[:, 3:4], z[:, 2:3], QMAX, r, ALU.mult, ALU.mult))
                link(nc.vector.tensor_scalar(xm[0:n, t % 2, :], dx[0:n, t % 2, :], z[:, 3:4], MAGIC,
                                             ALU.mult, ALU.add))
                if t >= 2:
                    dve.wait_ge(xqT_psum, t - 1)
                nc.vector.tensor_scalar(xq[0:n, t % 2, :], xm[0:n, t % 2, :], -MAGIC, None, ALU.add)\
                    .then_inc(xq_ready, 1)
                nc.vector.tensor_scalar(z[:, 4:5], z[:, 1:2], wdq[0:n, 0:1], None, ALU.mult)
                nc.vector.tensor_scalar(z[:, 5:6], z[:, 1:2], wdq[0:n, 1:2], None, ALU.mult)\
                    .then_inc(scale1_ready, 1)

            def gate_product(t):
                n = rows(t)
                if t >= 2:
                    dve.wait_ge(lifted, 6 + 2 * t - 2)
                for half in range(2):
                    dve.wait_ge(gu_psum, 2 * t + half + 1)
                    dve.wait_ge(sg_ready, 2 * t + half + 1)
                    nc.vector.tensor_tensor(g2[t % 2][0:n, half * 512:(half + 1) * 512],
                                            bank[3 + 2 * half][0:n, :],
                                            sg[0:n, t % 2, half * 512:(half + 1) * 512], ALU.mult)\
                        .then_inc(g2_ready, 1)

            def product_scale(t):
                n = rows(t)
                z = q1[0:n, t, :]
                z5 = z[:, 5:6]
                dve.wait_ge(g2_ready, 2 * t + 2)
                dve.wait_ge(scale1_ready, t + 1)
                link(nc.vector.tensor_reduce(z[:, 0:1], g2[t % 2][0:n, :], AX_X, ALU.max,
                                             apply_absolute_value=True))
                link(nc.vector.tensor_scalar(z[:, 6:7], z[:, 0:1], z5, 1e-5, ALU.mult, ALU.max))
                link(nc.vector.reciprocal(z[:, 2:3], z[:, 6:7]))
                nc.vector.tensor_scalar(z[:, 3:4], z[:, 2:3], QMAX, z5, ALU.mult, ALU.mult)\
                    .then_inc(scale2_ready, 1)
                link(nc.vector.tensor_scalar(z[:, 7:8], z[:, 6:7], wdq[0:n, 2:3], None, ALU.mult))

            def finish(t):
                n = rows(t)
                dve.wait_ge(d_psum, t + 1)
                nc.vector.scalar_tensor_tensor(out=o_sb[0:n, t, :], in0=bank[7][0:n, 0:C],
                                               scalar=q1[0:n, t, 7:8], in1=h_sb[0:n, t, :],
                                               op0=ALU.mult, op1=ALU.add).then_inc(out_ready, 1)

            def clip(i, half):
                v = tern[("gate", "up", "down")[i]][:, half * INNER:(half + 1) * INNER]
                dve.wait_ge(rounded, 2 * i + half + 1)
                nc.vector.tensor_scalar(v, v, 1.0, -1.0, ALU.min, ALU.max).then_inc(tern_ready, 1)

            nc.vector.memset(ones[:, :], 1.0).then_inc(ones_ready, 1)
            nc.vector.memset(mhalf[:, :], -0.5).then_inc(const_ready, 1)
            dve.wait_ge(ld_eyef, 16)
            nc.vector.tensor_copy(eyeb[:, :], eyef[:, :]).then_inc(const_ready, 1)
            dve.wait_ge(ld_cls, 16)
            variance(0)
            norm1(0)
            nc.vector.memset(vb[:, 0:B // 2, :], 0.0).then_inc(vb_zero, 1)
            dve.wait_ge(ld_pos, 16)
            dve.wait_ge(ld_b, 16)
            link(nc.vector.tensor_tensor(posb[:, :], pos_sb[:, :], b_sb[:, :], ALU.add))
            variance(1)
            variance(2)
            norm1(1)
            variance(3)
            norm1(2)
            variance(4)
            norm1(3)
            norm1(4)
            dve.wait_ge(ld_tab, 48)
            rotate(0)
            dve.wait_ge(kc_psum, 1)
            nc.vector.tensor_copy(kcls[:, :], bank[7][:, 0:2]).then_inc(kc_copied, 1)
            rotate(1)
            dve.wait_ge(kc_copied, 1)
            dve.wait_ge(kb_zero, 1)
            for j in range(2):
                for g in range(G):
                    ps = slice(g * HD, (g + 1) * HD)
                    last = nc.vector.tensor_copy(kb[ps, j, :, g * S],
                                                 kcls[ps, j:j + 1].broadcast_to([HD, B]))
            last.then_inc(kcls_placed, 1)
            rotate(2)
            dve.wait_ge(vT_psum, 1)
            nc.vector.tensor_copy(vT[:, :], bank[7][:, 0:2]).then_inc(vT_ready, 1)
            rotate(3)
            rotate(4)
            rotate(5)
            rotate(6)
            dve.wait_ge(tot_psum, 1)
            nc.vector.tensor_scalar(wm[:, :], bank[7][:, 0:3], 1.0 / (C * INNER), 1e-5,
                                    ALU.mult, ALU.max).then_inc(wm_ready, 1)
            dve.wait_ge(wm_ready, 1)
            nc.vector.reciprocal(wscale[:, :], wm[:, :]).then_inc(wscale_ready, 1)
            link(nc.vector.tensor_scalar(wdq[:, :], wm[:, :], 1.0 / QMAX, None, ALU.mult))
            mask_scores(1)
            rotate(7)
            clip(0, 0)
            mask_scores(2)
            sum_exps(1)
            rotate(8)
            clip(0, 1)
            rotate(9)
            sum_exps(2)
            clip(1, 0)
            clip(1, 1)
            mask_scores(3)
            norm2(0)
            clip(2, 0)
            mask_scores(4)
            clip(2, 1)
            sum_exps(3)
            sum_exps(4)
            norm2(1)
            gate_product(0)
            product_scale(0)
            norm2(2)
            gate_product(1)
            finish(0)
            product_scale(1)
            norm2(3)
            gate_product(2)
            finish(1)
            product_scale(2)
            norm2(4)
            gate_product(3)
            finish(2)
            product_scale(3)
            gate_product(4)
            finish(3)
            product_scale(4)
            finish(4)

        @block.scalar
        def _(act):
            def copy_yT(t):
                act.wait_ge(yT_psum, t + 1)
                nc.scalar.copy(yT[:, :, tcols(t)],
                               bank[4 + t % 2][:, 0:C].rearrange("p (c n) -> p c n", c=CC)[:, :, 0:rows(t)])\
                    .then_inc(yT_ready, 1)

            def copy_v(t):
                act.wait_ge(v_psum, t + 1)
                nc.scalar.copy(v_sb[0:rows(t), t, :], bank[6 + t % 2][0:rows(t), 0:C])\
                    .then_inc(v_ready, 1)

            def place_keys(half):
                act.wait_ge(kb_zero, 1)
                act.wait_ge(k_rotated, half + 1)
                bs = slice(half * B // 2, (half + 1) * B // 2)
                for j in range(2):
                    for g in range(G):
                        ps = slice(g * HD, (g + 1) * HD)
                        last = nc.scalar.copy(kb[ps, j, bs, g * S + 1:(g + 1) * S],
                                              kr[ps, j, :].rearrange("p (b n) -> p b n", n=N))
                last.then_inc(k_placed, 1)

            def round_weights(i):
                name = ("gate", "up", "down")[i]
                for half in range(2):
                    cols = slice(half * INNER, (half + 1) * INNER)
                    nc.scalar.activation(raw[name][:, cols], raw[name][:, cols], ACT.Identity,
                                         scale=wscale[:, i:i + 1], bias=magic[:, 0:1])\
                        .then_inc(lifted, 1)
                for half in range(2):
                    cols = slice(half * INNER, (half + 1) * INNER)
                    act.wait_ge(lifted, 2 * i + half + 1)
                    nc.scalar.activation(tern[name][:, cols], raw[name][:, cols], ACT.Identity,
                                         bias=magic[:, 1:2]).then_inc(rounded, 1)

            def exps(t):
                act.wait_ge(shifted, t)
                nc.scalar.activation(ex[:, t - 1, :], sc[:, t - 1, :], ACT.Exp, scale=SCALE)\
                    .then_inc(exp_done, 1)

            def copy_pT(t):
                act.wait_ge(pT_psum, t)
                if t >= 3:
                    act.wait_ge(o_psum, t - 2)
                nc.scalar.copy(pT[:, t % 2, :], bank[6][0:GK, :]).then_inc(pT_ready, 1)

            def copy_oT(t):
                if t >= 3:
                    act.wait_ge(a_psum, t - 1)
                for gp in range(2):
                    act.wait_ge(o_psum, 2 * t - 1 + gp)
                    nc.scalar.copy(
                        oT[:, t % 2, gp, :, :].rearrange("p r (b n) -> p b r n", n=N),
                        bank[gp][:, :].rearrange("p (b r n) -> p b r n", r=R, n=N))\
                        .then_inc(oT_ready, 1)

            def copy_xqT(t):
                act.wait_ge(xqT_psum, t + 1)
                if t >= 2:
                    act.wait_ge(gu_psum, 2 * t - 2)
                n = rows(t)
                nc.scalar.copy(xqT[:, t % 2, :, 0:n],
                               bankb[0][:, 0:C].rearrange("p (c n) -> p c n", c=CC)[:, :, 0:n])\
                    .then_inc(xqT_ready, 1)

            def silu(t):
                n = rows(t)
                act.wait_ge(scale1_ready, t + 1)
                for half in range(2):
                    act.wait_ge(gu_psum, 2 * t + half + 1)
                    if t >= 2:
                        act.wait_ge(g2_ready, 2 * t + half - 3)
                    nc.scalar.activation(sg[0:n, t % 2, half * 512:(half + 1) * 512],
                                         bank[2 + 2 * half][0:n, :], ACT.Silu,
                                         scale=q1[0:n, t, 4:5]).then_inc(sg_ready, 1)

            def lift_product(t):
                n = rows(t)
                act.wait_ge(scale2_ready, t + 1)
                for half in range(2):
                    cols = slice(half * 512, (half + 1) * 512)
                    if t:
                        act.wait_ge(g2q_ready, 2 * t + half - 1)
                    nc.scalar.activation(g2m[0:n, cols], g2[t % 2][0:n, cols], ACT.Identity,
                                         scale=q1[0:n, t, 3:4], bias=magic[0:n, 0:1])\
                        .then_inc(lifted, 1)

            def copy_g2T(t):
                act.wait_ge(g2T_psum, t + 1)
                if t >= 2:
                    act.wait_ge(d_psum, t - 1)
                n = rows(t)
                v = bankb[6].rearrange("p (c n) -> p c n", c=IC)
                for half in range(2):
                    cs = slice(half * IC // 2, (half + 1) * IC // 2)
                    nc.scalar.copy(g2T[:, t % 2, cs, 0:n], v[:, cs, 0:n]).then_inc(g2T_ready, 1)

            act.dma_start(wtok_sb[:, 0, :], w_tok[0]).then_inc(ld_x[0], 16)
            act.dma_start(eyef[:, :], eye_f).then_inc(ld_eyef, 16)
            act.dma_start(h_sb[0:1, 0, :], cls_tok).then_inc(ld_cls, 16)
            act.dma_start(b_sb[:, :], tok_b.broadcast_to([P, C])).then_inc(ld_b, 16)
            copy_yT(0)
            copy_v(0)
            copy_yT(1)
            copy_yT(2)
            copy_v(1)
            copy_v(2)
            copy_yT(3)
            copy_yT(4)
            place_keys(0)
            copy_v(3)
            copy_v(4)
            for i, (name, s) in enumerate((("gate", ld_gate), ("up", ld_up), ("down", ld_down))):
                act.wait_ge(s, 16)
                nc.scalar.activation(tern[name][:, :], raw[name][:, :], ACT.Abs,
                                     accum_out=asum[:, i:i + 1]).then_inc(abs_done, 1)
            place_keys(1)
            act.wait_ge(const_ready, 4)
            act.wait_ge(wscale_ready, 1)
            act.wait_ge(abs_done, 3)
            round_weights(0)
            exps(1)
            round_weights(1)
            exps(2)
            copy_pT(1)
            round_weights(2)
            copy_oT(1)
            exps(3)
            exps(4)
            copy_xqT(0)
            silu(0)
            copy_pT(2)
            copy_oT(2)
            lift_product(0)
            for t in range(2, TILES):
                copy_xqT(t - 1)
                copy_g2T(t - 2)
                silu(t - 1)
                copy_pT(t + 1)
                copy_oT(t + 1)
                lift_product(t - 1)
            copy_xqT(3)
            copy_g2T(2)
            silu(3)
            lift_product(3)
            copy_xqT(4)
            copy_g2T(3)
            silu(4)
            lift_product(4)
            copy_g2T(4)

        @block.gpsimd
        def _(pool):
            def inv_std(t, i, ready, done):
                n = rows(t)
                pool.wait_ge(ready, t + 1)
                nc.gpsimd.tensor_tensor(rstd[0:n, t, i, 1:2], rstd[0:n, t, i, 0:1], mhalf[0:n, :],
                                        ALU.pow).then_inc(done, 1)

            def combine(s):
                half, r = divmod(s, R + 1)
                pool.wait_ge(proj_read, s + 1)
                a, b = rc[:, s % 2, :, :], rs[:, s % 2, :, :]
                bs = slice(half * B // 2, (half + 1) * B // 2)
                for j, left, right, op in ((0, a[:, 0, :], b[:, 1, :], ALU.subtract),
                                           (1, b[:, 0, :], a[:, 1, :], ALU.add)):
                    last = nc.gpsimd.tensor_tensor(
                        qr[:, j, bs, r - 1, :], left.rearrange("p (b n) -> p b n", n=N),
                        right.rearrange("p (b n) -> p b n", n=N), op)
                last.then_inc(roped, 1)

            def shift(t):
                pool.wait_ge(smax_ready, t)
                v = sc[:, t - 1, :].rearrange("p (a k) -> p a k", k=S)
                nc.gpsimd.tensor_tensor(v, v, smax[:, t - 1, :].unsqueeze(2)
                                        .broadcast_to([P, PAIRS * G, S]), ALU.subtract)\
                    .then_inc(shifted, 1)

            def normalise(t):
                pool.wait_ge(srec_ready, t)
                v = ex[:, t - 1, :].rearrange("p (a k) -> p a k", k=S)
                nc.gpsimd.tensor_tensor(v, v, srec[:, t - 1, :].unsqueeze(2)
                                        .broadcast_to([P, PAIRS * G, S]), ALU.mult)\
                    .then_inc(probs_ready, 1)

            def round_product(t):
                n = rows(t)
                if t >= 2:
                    pool.wait_ge(g2T_psum, t - 1)
                for half in range(2):
                    cols = slice(half * 512, (half + 1) * 512)
                    pool.wait_ge(lifted, 6 + 2 * t + half + 1)
                    nc.gpsimd.tensor_scalar(g2q[0:n, t % 2, cols], g2m[0:n, cols], 1.0, -MAGIC,
                                            ALU.mult, ALU.add).then_inc(g2q_ready, 1)

            nc.gpsimd.memset(kb[:, :, :, :], 0.0).then_inc(kb_zero, 1)
            nc.gpsimd.memset(magic[:, 0:1], MAGIC).then_inc(const_ready, 1)
            nc.gpsimd.memset(magic[:, 1:2], -MAGIC).then_inc(const_ready, 1)
            pool.wait_ge(const_ready, 4)
            inv_std(0, 0, var_ready, rstd_ready)
            nc.gpsimd.memset(vb[:, B // 2:B, :], 0.0).then_inc(vb_zero, 1)
            for t in PATCH:
                inv_std(t, 0, var_ready, rstd_ready)
            for s in (1, 2, 3, 4, 6, 7):
                combine(s)
            shift(1)
            shift(2)
            normalise(1)
            combine(8)
            combine(9)
            normalise(2)
            pool.wait_ge(ld_wo, 16)
            steps = 0
            for a, b in ((wo_sb[:, :, 0, :], wo_sb[:, :, 1, :]), (wo_sum, wo_sb[:, :, 2, :]),
                         (wo_sum, wo_sb[:, :, 3, :])):
                if steps:
                    pool.wait_ge(pool_link, steps)
                ins = nc.gpsimd.tensor_tensor(wo_sum[:, :, :], a[:, :, :], b[:, :, :], ALU.add)
                steps += 1
                ins.then_inc(pool_link if steps < 3 else wo_summed, 1)
            shift(3)
            inv_std(0, 1, var2_ready, rstd2_ready)
            shift(4)
            normalise(3)
            normalise(4)
            inv_std(1, 1, var2_ready, rstd2_ready)
            for t in range(2, TILES + 1):
                round_product(t - 2)
                inv_std(t, 1, var2_ready, rstd2_ready)
            round_product(3)
            round_product(4)


def shape_constants():
    import numpy as np
    inv = (1.0 / np.float32(10000.0) ** (np.arange(0, D, 2, dtype=np.float32) / np.float32(D)))
    ang = np.arange(1, S, dtype=np.float32)[None, :] * inv.astype(np.float32)[:, None]
    cos_t = np.tile(np.cos(ang).astype(np.float32), (G, 1))
    sin_t = np.tile(np.sin(ang).astype(np.float32), (G, 1))
    q = np.arange(P)[:, None] % N + 1
    mask_t = np.where(np.arange(S)[None, :] <= q, 0.0, MASKED).astype(np.float32)
    return {"cos_t": cos_t, "sin_t": sin_t, "mask_t": mask_t,
            "eye_f": np.eye(P, dtype=np.float32)}


def kernel(**inputs):
    import numpy as np
    import concourse.bacc as bacc
    from concourse.bass_utils import run_bass_kernel_spmd

    a = {k: np.asarray(v) for k, v in inputs.items()}
    ps = 16
    lay = {
        "xT": a["x"].reshape(B, 3, 4, ps, 4, ps).transpose(1, 3, 5, 0, 2, 4).reshape(FC, P, TOK),
        "w_tok": a["L0_tok_W"].T.reshape(FC, P, C),
        "tok_b": a["L0_tok_b"].reshape(1, C),
        "pos": np.tile(a["L0_tok_pos_emb"], (TI, 1)),
        "cls_tok": a["cls_tok"].reshape(1, C),
        "wq": a["L0_attn_Wq"].reshape(CC, P, G, R, HD, 2).transpose(1, 0, 3, 5, 2, 4)
                             .reshape(P, CC, R, 2, P),
        "wk": a["L0_attn_Wk"].reshape(CC, P, G, HD, 2).transpose(1, 0, 4, 2, 3).reshape(P, CC, 2, P),
        "wv": a["L0_attn_Wv"].reshape(CC, P, C).transpose(1, 0, 2),
        "wo": a["L0_attn_Wo"].reshape(2, 2, R, D, C).transpose(1, 3, 0, 2, 4).reshape(P, 2, R, C),
        "w_gate": a["L0_ffn_w_gate"].T.reshape(CC, P, INNER).transpose(1, 0, 2).reshape(P, 2 * INNER),
        "w_up": a["L0_ffn_w_up"].T.reshape(CC, P, INNER).transpose(1, 0, 2).reshape(P, 2 * INNER),
        "w_down": a["L0_ffn_w_down"].T.reshape(IC, P, C).transpose(1, 0, 2).reshape(P, 2 * INNER),
    }
    lay.update(shape_constants())

    nc = bacc.Bacc("TRN2", target_bir_lowering=False, num_devices=1)
    arrays, args = {}, {}
    for name, v in lay.items():
        v = np.ascontiguousarray(v)
        arrays[f"in_{name}"] = v
        args[name] = nc.dram_tensor(f"in_{name}", v.shape, mybir.dt.from_np(v.dtype),
                                    kind="ExternalInput").ap()
    out = nc.dram_tensor("out_0", (B, S, C), F32, kind="ExternalOutput").ap()
    build(nc, out=out, **args)
    r = run_bass_kernel_spmd(nc, [arrays], core_ids=[0])
    return r.results[0]["out_0"]
```

```python
from contextlib import ExitStack

import concourse.bass as bass
from concourse import mybir

ALU = mybir.AluOpType
ACT = mybir.ActivationFunctionType
F32 = mybir.dt.float32
BF16 = mybir.dt.bfloat16
AX_X = mybir.AxisListType.X

P = 128
B = 32
N = 16
S = N + 1
C = 256
CC = C // P
IN_FEAT = 768
FC = IN_FEAT // P
G, R, D = 4, 4, 64
HD = D // 2
INNER = 1024
IC = INNER // P
TOK = B * N
TILES = TOK // P
TI = P // N
PAIRS = TI // 2
HALF = TOK // 2
GK = G * S
EPS = 1e-5
MASKED = -1e30
MAGIC = 1.5 * 2.0 ** 23
QMAX = 127.0
SCALE = float(D) ** -0.5
XQ_BANK = (3, 0, 0, 0, 0)
DOWN_BANK = (7, 7, 1, 7, 1)
ORDER = (0, 1, 2, 3, 4)
BY_TILE = 3
WARM = 9


def build(nc, xT, w_tok, tok_b, pos, cls_tok, wq, wk, wv, wo, w_gate, w_up, w_down,
          cos_t, sin_t, mask_t, eye_f, out):
    with ExitStack() as ctx:
        def sb(name, shape, dt=F32):
            return ctx.enter_context(nc.sbuf_tensor(name, shape, dt))

        def sem(name):
            return ctx.enter_context(nc.semaphore(name))

        x_sb = sb("x_sb", [P, FC, TOK])
        wtok_sb = sb("wtok_sb", [P, FC, C])
        b_sb = sb("b_sb", [P, C])
        pos_sb = sb("pos_sb", [P, C])
        posb = sb("posb", [P, C])
        wq_sb = sb("wq_sb", [P, CC, R, 2, P])
        wk_sb = sb("wk_sb", [P, CC, 2, P])
        wv_sb = sb("wv_sb", [P, CC, C])
        wo_sb = sb("wo_sb", [P, 2, R, C])
        wo_sum = sb("wo_sum", [P, 2, C])
        raw = {n: sb(f"raw_{n}", [P, 2 * INNER]) for n in ("gate", "up", "down")}
        tern = {n: sb(f"tern_{n}", [P, 2 * INNER], BF16) for n in ("gate", "up", "down")}
        cos_sb = sb("cos_sb", [P, N])
        sin_sb = sb("sin_sb", [P, N])
        mask_sb = sb("mask_sb", [P, S])
        eyef = sb("eyef", [P, P])
        eyeb = sb("eyeb", [P, P], BF16)
        ones = sb("ones", [P, P])
        mhalf = sb("mhalf", [P, 1])
        magic = sb("magic", [P, 2])
        h_sb = sb("h_sb", [P, TILES + 1, C])
        y_sb = sb("y_sb", [P, 2, C])
        yT = sb("yT", [P, CC, TOK + 1])
        stats = sb("stats", [P, TILES + 1, 2, 8])
        rstd = sb("rstd", [P, TILES + 1, 2, 2])
        rc = sb("rc", [P, 2, 2, HALF])
        rs = sb("rs", [P, 2, 2, HALF])
        kr = sb("kr", [P, 2, HALF])
        qr = sb("qr", [P, 2, B, R, N])
        kb = sb("kb", [P, 2, B, GK])
        kcls = sb("kcls", [P, 2])
        v_sb = sb("v_sb", [P, TILES + 1, C])
        vb = sb("vb", [GK, B, C])
        vT = sb("vT", [P, 2])
        sc = sb("sc", [P, TILES, PAIRS * GK])
        ex = sb("ex", [P, TILES, PAIRS * GK])
        smax = sb("smax", [P, TILES, PAIRS * G])
        ssum = sb("ssum", [P, TILES, PAIRS * G])
        srec = sb("srec", [P, TILES, PAIRS * G])
        pT = sb("pT", [GK, 2, PAIRS * P])
        oT = sb("oT", [P, 2, 2, R, P])
        asum = sb("asum", [P, 4])
        wm = sb("wm", [P, 3])
        wscale = sb("wscale", [P, 3])
        wdq = sb("wdq", [P, 3])
        q1 = sb("q1", [P, TILES + 1, 8])
        ahead = sb("ahead", [P, 1])
        dx = sb("dx", [P, 2, C])
        xm = sb("xm", [P, 2, C])
        xq = sb("xq", [P, 2, C], BF16)
        xqT = sb("xqT", [P, 2, CC, P], BF16)
        sg = x_sb[:, 0:4, :].rearrange("p (a b) n -> p a (b n)", a=2)
        g2 = (x_sb[:, 4:6, :].rearrange("p a n -> p (a n)"),
              wtok_sb[:, 0:4, :].rearrange("p a n -> p (a n)"))
        g2m = rc[:, :, :, :].rearrange("p a j n -> p (a j n)")
        g2q = sb("g2q", [P, 2, INNER], BF16)
        g2T = sb("g2T", [P, 2, IC, P], BF16)
        o_sb = h_sb
        v_dram = nc.dram_tensor("v_scratch", [TOK + 1, C], F32, kind="Internal").ap()

        bank = [ctx.enter_context(nc.psum_tensor(f"bank{i}", [P, 512], F32)) for i in range(8)]
        bankb = [b[:, :].bitcast(BF16) for b in bank]

        ld_cls, ld_pos, ld_b, ld_eyef, ld_tab = (sem(n) for n in (
            "ld_cls", "ld_pos", "ld_b", "ld_eyef", "ld_tab"))
        ld_x = [sem(f"ld_x{c}") for c in range(FC)]
        ld_wk, ld_wv, ld_wo, ld_gate, ld_up, ld_down = (sem(n) for n in (
            "ld_wk", "ld_wv", "ld_wo", "ld_gate", "ld_up", "ld_down"))
        ld_wq = [sem(f"ld_wq{c}") for c in range(2)]
        v_stored = sem("v_stored")
        vb_loaded = [sem(f"vb_loaded{h}") for h in range(3)]
        stored = sem("stored")
        const_ready, kb_zero, vb_zero = sem("const_ready"), sem("kb_zero"), sem("vb_zero")
        ones_ready = sem("ones_ready")
        embedded, posb_ready, h_ready = sem("embedded"), sem("posb_ready"), sem("h_ready")
        dve_link, pool_link, act_link = sem("dve_link"), sem("pool_link"), sem("act_link")
        var_ready, rstd_ready, y_ready = sem("var_ready"), sem("rstd_ready"), sem("y_ready")
        yT_psum, yT_ready = sem("yT_psum"), sem("yT_ready")
        v_psum, v_ready = sem("v_psum"), sem("v_ready")
        kc_psum, kc_copied = sem("kc_psum"), sem("kc_copied")
        vT_psum, vT_ready = sem("vT_psum"), sem("vT_ready")
        proj_psum, proj_read, roped = sem("proj_psum"), sem("proj_read"), sem("roped")
        kcls_placed, k_rotated, k_placed = sem("kcls_placed"), sem("k_rotated"), sem("k_placed")
        abs_done, tot_psum, wm_ready, tern_ready = (sem(n) for n in (
            "abs_done", "tot_psum", "wm_ready", "tern_ready"))
        wscale_ready, lifted, rounded = sem("wscale_ready"), sem("lifted"), sem("rounded")
        wo_summed = sem("wo_summed")
        s_psum, s_read, smax_ready, shifted, exp_done = (sem(n) for n in (
            "s_psum", "s_read", "smax_ready", "shifted", "exp_done"))
        srec_ready, probs_ready, pT_psum, pT_ready = (sem(n) for n in (
            "srec_ready", "probs_ready", "pT_psum", "pT_ready"))
        o_psum, oT_ready, a_psum, h1_ready = (sem(n) for n in (
            "o_psum", "oT_ready", "a_psum", "h1_ready"))
        var2_ready, rstd2_ready, xq_ready, xqT_psum, xqT_ready = (sem(n) for n in (
            "var2_ready", "rstd2_ready", "xq_ready", "xqT_psum", "xqT_ready"))
        gu_psum, sg_ready, g2_ready, g2m_ready, g2q_ready, g2T_psum, g2T_ready = (sem(n) for n in (
            "gu_psum", "sg_ready", "g2_ready", "g2m_ready", "g2q_ready", "g2T_psum", "g2T_ready"))
        g2q_last, g2T_last = sem("g2q_last"), sem("g2T_last")
        scale1_ready, scale2_ready = sem("scale1_ready"), sem("scale2_ready")
        d_psum, out_ready = sem("d_psum"), sem("out_ready")

        block = ctx.enter_context(nc.Block())

        def rows(t):
            return 1 if t == 0 else P

        def tcols(t):
            return slice(TOK, TOK + 1) if t == 0 else slice((t - 1) * P, t * P)

        def combined(s):
            return s - s // (R + 1)

        ALL = range(TILES + 1)
        PATCH = range(1, TILES + 1)

        @block.sync
        def _(sp):
            for c in range(FC):
                sp.dma_start(x_sb[:, c, :], xT[c]).then_inc(ld_x[c], 16)
                if c:
                    sp.dma_start(wtok_sb[:, c, :], w_tok[c]).then_inc(ld_x[c], 16)
            sp.dma_start(pos_sb[:, :], pos).then_inc(ld_pos, 16)
            sp.dma_start(wv_sb[:, :, :], wv).then_inc(ld_wv, 16)
            sp.dma_start(wk_sb[:, :, :, :], wk).then_inc(ld_wk, 16)
            sp.dma_start(cos_sb[:, :], cos_t).then_inc(ld_tab, 16)
            sp.dma_start(sin_sb[:, :], sin_t).then_inc(ld_tab, 16)
            sp.dma_start(mask_sb[:, :], mask_t).then_inc(ld_tab, 16)
            for c in range(2):
                sp.dma_start(wq_sb[:, :, 2 * c:2 * c + 2, :, :], wq[:, :, 2 * c:2 * c + 2, :, :])\
                    .then_inc(ld_wq[c], 16)
            sp.dma_start(wo_sb[:, :, :, :], wo).then_inc(ld_wo, 16)
            sp.dma_start(raw["gate"][:, :], w_gate).then_inc(ld_gate, 16)
            sp.dma_start(raw["up"][:, :], w_up).then_inc(ld_up, 16)
            sp.dma_start(raw["down"][:, :], w_down).then_inc(ld_down, 16)

            for t in ALL:
                sp.wait_ge(v_ready, t + 1)
                dst = v_dram[TOK:TOK + 1, :] if t == 0 else v_dram[(t - 1) * P:t * P, :]
                sp.dma_start(dst, v_sb[0:rows(t), t, :]).then_inc(v_stored, 16)
            sp.wait_ge(vb_zero, 2)
            sp.wait_ge(v_stored, 16 * (TILES + 1))
            vg = v_dram[0:TOK, :].rearrange("(b n) (g d) -> g n b d", n=N, g=G)
            for g in range(G):
                sp.dma_start(vb[g * S:g * S + 1, :, g * D:(g + 1) * D],
                             v_dram[TOK:TOK + 1, g * D:(g + 1) * D].unsqueeze(1)
                             .broadcast_to([1, B, D])).then_inc(vb_loaded[0], 16)
            for half in range(2):
                bs = slice(half * B // 2, (half + 1) * B // 2)
                for g in range(G):
                    sp.dma_start(vb[g * S + 1:(g + 1) * S, bs, g * D:(g + 1) * D],
                                 vg[g, :, bs, :]).then_inc(vb_loaded[1 + half], 16)
            for k, t in enumerate(ORDER):
                sp.wait_ge(out_ready, k + 1)
                if t == 0:
                    sp.dma_start(out[:, 0:1, :].rearrange("b s c -> s b c"),
                                 o_sb[0:1, 0, :].unsqueeze(1).broadcast_to([1, B, C]))\
                        .then_inc(stored, 16)
                else:
                    sp.dma_start(out[(t - 1) * TI:t * TI, 1:S, :], o_sb[:, t, :]).then_inc(stored, 16)
            sp.wait_ge(stored, 16 * (TILES + 1))

        @block.tensor
        def _(pe):
            def transpose_y(t):
                pe.wait_ge(y_ready, t + 1)
                if t >= 2:
                    pe.wait_ge(yT_ready, t - 1)
                n = rows(t)
                for c in range(CC):
                    last = nc.tensor.transpose(bank[4 + t % 2][:, c * P:c * P + n],
                                               y_sb[0:n, t % 2, c * P:(c + 1) * P], eyef[0:n, 0:n])
                last.then_inc(yT_psum, 1)

            def values(t):
                pe.wait_ge(yT_ready, t + 1)
                if t >= 2:
                    pe.wait_ge(v_ready, t - 1)
                if t == 3:
                    pe.wait_ge(kc_copied, 1)
                for c in range(CC):
                    last = nc.tensor.matmul(bank[6 + t % 2][0:rows(t), 0:C], yT[:, c, tcols(t)],
                                            wv_sb[:, c, :], start=c == 0, stop=c == CC - 1)
                last.then_inc(v_psum, 1)

            def project(s):
                half, r = divmod(s, R + 1)
                w = wk_sb[:, :, :, :] if r == 0 else wq_sb[:, :, r - 1, :, :]
                if s < 4:
                    pe.wait_ge(h_ready, s + 1)
                else:
                    pe.wait_ge(proj_read, s - 3)
                pe.wait_ge(yT_ready, 3 + 2 * half)
                for j in range(2):
                    for c in range(CC):
                        last = nc.tensor.matmul(bank[s % 4][:, j * HALF:(j + 1) * HALF], w[:, c, j, :],
                                                yT[:, c, half * HALF:(half + 1) * HALF],
                                                start=c == 0, stop=c == CC - 1)
                last.then_inc(proj_psum, 1)

            def scores(t):
                half = (t - 1) // 2
                pe.wait_ge(k_placed, half + 1)
                pe.wait_ge(roped, R * (half + 1))
                if t == 1:
                    pe.wait_ge(kcls_placed, 1)
                if t <= 2:
                    pe.wait_ge(yT_ready, 3 + t)
                else:
                    pe.wait_ge(s_read, t - 2)
                for b in range(TI):
                    img, row = (t - 1) * TI + b, b % 2 * D
                    for j in range(2):
                        last = nc.tensor.matmul(
                            bank[4 + t % 2][row:row + D, b // 2 * GK:(b // 2 + 1) * GK],
                            qr[:, j, img, :, :].rearrange("p r n -> p (r n)"), kb[:, j, img, :],
                            start=j == 0, stop=j == 1)
                last.then_inc(s_psum, 1)

            def transpose_probs(t, free):
                pe.wait_ge(*free)
                pe.wait_ge(probs_ready, t)
                for pr in range(PAIRS):
                    last = nc.tensor.transpose(bank[6][0:GK, pr * P:(pr + 1) * P],
                                               ex[:, t - 1, pr * GK:(pr + 1) * GK], eyef[:, :])
                last.then_inc(pT_psum, 1)

            def mix(t, xq_before=0):
                if xq_before:
                    pe.wait_ge(xqT_ready, xq_before)
                pe.wait_ge(pT_ready, t)
                if t == 1:
                    pe.wait_ge(vb_loaded[0], 16 * G)
                if t % 2:
                    pe.wait_ge(vb_loaded[1 + t // 2], 16 * G)
                for gp in range(2):
                    if t == 1:
                        pe.wait_ge(proj_read, 9 + gp)
                    else:
                        pe.wait_ge(oT_ready, 2 * t - 3 + gp)
                    for b in range(TI):
                        last = nc.tensor.matmul(
                            bank[gp][:, b * D:(b + 1) * D],
                            vb[:, (t - 1) * TI + b, gp * P:(gp + 1) * P],
                            pT[:, t % 2, b * D:(b + 1) * D], start=True, stop=True)
                    last.then_inc(o_psum, 1)

            def attend_out(t, free):
                pe.wait_ge(*free)
                if t == 0:
                    pe.wait_ge(wo_summed, 1)
                    pe.wait_ge(vT_ready, 1)
                    for gp in range(2):
                        last = nc.tensor.matmul(bank[7][0:1, 0:C], vT[:, gp:gp + 1], wo_sum[:, gp, :],
                                                start=gp == 0, stop=gp == 1)
                else:
                    for k in range(2 * R):
                        if k % R == 0:
                            pe.wait_ge(oT_ready, 2 * t - 1 + k // R)
                        last = nc.tensor.matmul(bank[7][:, 0:C], oT[:, t % 2, k // R, k % R, :],
                                                wo_sb[:, k // R, k % R, :],
                                                start=k == 0, stop=k == 2 * R - 1)
                last.then_inc(a_psum, 1)

            def transpose_xq(k, free):
                pe.wait_ge(*free)
                pe.wait_ge(xq_ready, k + 1)
                n = rows(ORDER[k])
                for c in range(CC):
                    last = nc.tensor.transpose(bankb[XQ_BANK[k]][:, c * P:c * P + n],
                                               xq[0:n, k % 2, c * P:(c + 1) * P], eyeb[0:n, 0:n])
                last.then_inc(xqT_psum, 1)

            def gate_up(k):
                n = rows(ORDER[k])
                pe.wait_ge(xqT_ready, k + 1)
                if k == 0:
                    pe.wait_ge(proj_read, 8)
                    pe.wait_ge(tern_ready, 4)
                for half in range(2):
                    if k:
                        pe.wait_ge(g2_ready, 2 * k + half - 1)
                    elif half:
                        pe.wait_ge(s_read, TILES)
                    for i, name in enumerate(("gate", "up")):
                        for c in range(CC):
                            col = c * INNER + half * 512
                            last = nc.tensor.matmul(bank[2 + 2 * half + i][0:n, :],
                                                    xqT[:, k % 2, c, 0:n],
                                                    tern[name][:, col:col + 512],
                                                    start=c == 0, stop=c == CC - 1)
                    last.then_inc(gu_psum, 1)

            def transpose_g2(k, free):
                pe.wait_ge(*free)
                n = rows(ORDER[k])
                for half in range(2):
                    pe.wait_ge(g2q_ready, 2 * k + half + 1)
                    for c in range(half * IC // 2, (half + 1) * IC // 2):
                        last = nc.tensor.transpose(bankb[6][:, c * P:c * P + n],
                                                   g2q[0:n, k % 2, c * P:(c + 1) * P], eyeb[0:n, 0:n])
                    last.then_inc(g2T_psum, 1)

            def transpose_last_g2():
                for half, bank_no, free, done in ((0, 6, (g2T_ready, 8), (g2q_last, 1)),
                                                  (1, 2, (g2_ready, 2 * TILES + 1), (g2q_ready, 2 * TILES + 1))):
                    pe.wait_ge(*free)
                    pe.wait_ge(*done)
                    for c in range(IC // 2):
                        last = nc.tensor.transpose(bankb[bank_no][:, c * P:(c + 1) * P],
                                                   g2q[:, 0, half * 512 + c * P:half * 512 + (c + 1) * P],
                                                   eyeb[:, :])
                    last.then_inc(g2T_psum, 1)

            def down(k, free):
                pe.wait_ge(*free)
                n = rows(ORDER[k])
                if k == 0:
                    pe.wait_ge(tern_ready, 6)
                for c in range(IC):
                    if c == IC // 2 and k == TILES:
                        pe.wait_ge(g2T_last, 1)
                    elif c % (IC // 2) == 0:
                        pe.wait_ge(g2T_ready, 2 * k + 1 + c // (IC // 2))
                    last = nc.tensor.matmul(bank[DOWN_BANK[k]][0:n, 0:C], g2T[:, k % 2, c, 0:n],
                                            tern["down"][:, c * C:(c + 1) * C],
                                            start=c == 0, stop=c == IC - 1)
                last.then_inc(d_psum, 1)

            pe.wait_ge(ones_ready, 1)
            for _ in range(WARM):
                nc.tensor.matmul(bank[7][:, 0:P], ones[:, :], ones[:, :], start=True, stop=True)
            for c in range(FC - BY_TILE):
                pe.wait_ge(ld_x[c], 32)
                for t in PATCH:
                    nc.tensor.matmul(bank[t - 1][:, 0:C], x_sb[:, c, tcols(t)], wtok_sb[:, c, :],
                                     start=c == 0, stop=False)
            pe.wait_ge(ld_eyef, 16)
            transpose_y(0)
            for t in PATCH:
                for c in range(FC - BY_TILE, FC):
                    if t == 1:
                        pe.wait_ge(ld_x[c], 32)
                    last = nc.tensor.matmul(bank[t - 1][:, 0:C], x_sb[:, c, tcols(t)],
                                            wtok_sb[:, c, :], start=False, stop=c == FC - 1)
                last.then_inc(embedded, 1)
            pe.wait_ge(ld_wv, 16)
            values(0)
            transpose_y(1)
            transpose_y(2)
            pe.wait_ge(ld_wk, 16)
            values(1)
            project(0)
            values(2)
            pe.wait_ge(v_ready, 2)
            for j in range(2):
                for c in range(CC):
                    last = nc.tensor.matmul(bank[7][:, j:j + 1], wk_sb[:, c, j, :],
                                            yT[:, c, TOK:TOK + 1], start=c == 0, stop=c == CC - 1)
            last.then_inc(kc_psum, 1)
            transpose_y(3)
            pe.wait_ge(ld_wq[0], 16)
            project(1)
            transpose_y(4)
            project(2)
            values(3)
            values(4)
            pe.wait_ge(v_ready, 4)
            for gp in range(2):
                last = nc.tensor.transpose(bank[7][:, gp:gp + 1], v_sb[0:1, 0, gp * P:(gp + 1) * P],
                                           eyef[0:1, 0:1])
            last.then_inc(vT_psum, 1)
            pe.wait_ge(ld_wq[1], 16)
            project(3)
            project(4)
            project(5)
            project(6)
            pe.wait_ge(abs_done, 3)
            pe.wait_ge(vT_ready, 1)
            nc.tensor.matmul(bank[7][:, 0:3], ones[:, :], asum[:, 0:3], start=True, stop=True)\
                .then_inc(tot_psum, 1)
            scores(1)
            project(7)
            scores(2)
            project(8)
            transpose_probs(1, (v_ready, TILES + 1))
            project(9)
            mix(1)
            scores(3)
            transpose_probs(2, (pT_ready, 1))
            attend_out(0, (wm_ready, 1))
            scores(4)
            pe.wait_ge(ld_wo, 16)
            pe.wait_ge(const_ready, 4)
            attend_out(1, (h1_ready, 1))
            transpose_xq(0, (proj_read, 9))
            mix(2)
            gate_up(0)
            transpose_probs(3, (pT_ready, 2))
            transpose_xq(1, (oT_ready, 3))
            attend_out(2, (h1_ready, 2))
            gate_up(1)
            mix(3, xq_before=2)
            transpose_xq(2, (oT_ready, 5))
            attend_out(3, (h1_ready, 3))
            transpose_g2(0, (pT_ready, 3))
            gate_up(2)
            transpose_probs(4, (g2T_ready, 2))
            down(0, (h1_ready, 4))
            transpose_g2(1, (pT_ready, 4))
            mix(4, xq_before=3)
            transpose_xq(3, (oT_ready, 7))
            down(1, (out_ready, 1))
            gate_up(3)
            transpose_g2(2, (g2T_ready, 4))
            attend_out(4, (out_ready, 2))
            down(2, (oT_ready, 8))
            transpose_g2(3, (g2T_ready, 6))
            down(3, (h1_ready, 5))
            transpose_xq(4, (xqT_ready, 4))
            gate_up(4)
            transpose_last_g2()
            down(4, (out_ready, 3))

        @block.vector
        def _(dve):
            links = [0]

            def link(ins):
                links[0] += 1
                ins.then_inc(dve_link, 1)
                dve.wait_ge(dve_link, links[0])

            def variance(t):
                n = rows(t)
                st = stats[0:n, t, 0, :]
                if t:
                    dve.wait_ge(embedded, t)
                    nc.vector.tensor_tensor(h_sb[:, t, :], bank[t - 1][:, 0:C], posb[:, :], ALU.add)\
                        .then_inc(h_ready, 1)
                    dve.wait_ge(h_ready, t)
                link(nc.vector.bn_stats(st[:, 0:6], h_sb[0:n, t, :]))
                link(nc.vector.bn_aggr(st[:, 6:8], st[:, 0:6]))
                nc.vector.tensor_scalar(rstd[0:n, t, 0, 0:1], st[:, 7:8], EPS, None, ALU.add)\
                    .then_inc(var_ready, 1)

            def norm1(t):
                n = rows(t)
                dve.wait_ge(rstd_ready, t + 1)
                if t >= 2:
                    dve.wait_ge(yT_psum, t - 1)
                nc.vector.tensor_scalar(y_sb[0:n, t % 2, :], h_sb[0:n, t, :], stats[0:n, t, 0, 6:7],
                                        rstd[0:n, t, 0, 1:2], ALU.subtract, ALU.mult)\
                    .then_inc(y_ready, 1)

            def rotate(s):
                dve.wait_ge(proj_psum, s + 1)
                if s >= 2 and combined(s - 2):
                    dve.wait_ge(roped, combined(s - 2))
                x = bank[s % 4][:, :].rearrange("p (a n) -> p a n", n=N)
                for dst, tab in ((rc, cos_sb), (rs, sin_sb)):
                    last = nc.vector.tensor_tensor(
                        dst[:, s % 2, :, :].rearrange("p j (b n) -> p (j b) n", n=N), x,
                        tab[:, :].unsqueeze(1).broadcast_to([P, 2 * HALF // N, N]), ALU.mult)
                last.then_inc(proj_read, 1)
                if s % (R + 1):
                    return
                half = s // (R + 1)
                dve.wait_ge(proj_read, s + 1)
                if half:
                    dve.wait_ge(k_placed, half)
                nc.vector.tensor_tensor(kr[:, 0, :], rc[:, s % 2, 0, :], rs[:, s % 2, 1, :],
                                        ALU.subtract)
                nc.vector.tensor_tensor(kr[:, 1, :], rs[:, s % 2, 0, :], rc[:, s % 2, 1, :],
                                        ALU.add).then_inc(k_rotated, 1)

            def mask_scores(t):
                dve.wait_ge(s_psum, t)
                v = sc[:, t - 1, :].rearrange("p (a k) -> p a k", k=S)
                nc.vector.tensor_tensor(
                    v, bank[4 + t % 2][:, 0:PAIRS * GK].rearrange("p (a k) -> p a k", k=S),
                    mask_sb[:, :].unsqueeze(1).broadcast_to([P, PAIRS * G, S]), ALU.add)\
                    .then_inc(s_read, 1)
                dve.wait_ge(s_read, t)
                nc.vector.tensor_reduce(smax[:, t - 1, :], v, AX_X, ALU.max).then_inc(smax_ready, 1)

            def sum_exps(t):
                dve.wait_ge(exp_done, t)
                link(nc.vector.tensor_reduce(ssum[:, t - 1, :],
                                             ex[:, t - 1, :].rearrange("p (a k) -> p a k", k=S),
                                             AX_X, ALU.add))
                nc.vector.reciprocal(srec[:, t - 1, :], ssum[:, t - 1, :]).then_inc(srec_ready, 1)

            def norm2(k):
                t = ORDER[k]
                n = rows(t)
                st = stats[0:n, t, 1, :]
                z = q1[0:n, t, :]
                dve.wait_ge(a_psum, k + 1)
                nc.vector.tensor_tensor(h_sb[0:n, t, :], bank[7][0:n, 0:C], h_sb[0:n, t, :], ALU.add)\
                    .then_inc(h1_ready, 1)
                dve.wait_ge(h1_ready, k + 1)
                link(nc.vector.bn_stats(st[:, 0:6], h_sb[0:n, t, :]))
                link(nc.vector.bn_aggr(st[:, 6:8], st[:, 0:6]))
                nc.vector.tensor_scalar(rstd[0:n, t, 1, 0:1], st[:, 7:8], EPS, None, ALU.add)\
                    .then_inc(var2_ready, 1)
                link(nc.vector.tensor_scalar(dx[0:n, k % 2, :], h_sb[0:n, t, :], st[:, 6:7], None,
                                             ALU.subtract))
                link(nc.vector.tensor_reduce(z[:, 0:1], dx[0:n, k % 2, :], AX_X, ALU.max,
                                             apply_absolute_value=True))
                dve.wait_ge(rstd2_ready, k + 1)
                r = rstd[0:n, t, 1, 1:2]
                link(nc.vector.tensor_scalar(z[:, 1:2], z[:, 0:1], r, 1e-5, ALU.mult, ALU.max))
                link(nc.vector.reciprocal(z[:, 2:3], z[:, 1:2]))
                link(nc.vector.tensor_scalar(z[:, 3:4], z[:, 2:3], QMAX, r, ALU.mult, ALU.mult))
                link(nc.vector.tensor_scalar(xm[0:n, k % 2, :], dx[0:n, k % 2, :], z[:, 3:4], MAGIC,
                                             ALU.mult, ALU.add))
                if k >= 2:
                    dve.wait_ge(xqT_psum, k - 1)
                nc.vector.tensor_scalar(xq[0:n, k % 2, :], xm[0:n, k % 2, :], -MAGIC, None, ALU.add)\
                    .then_inc(xq_ready, 1)
                nc.vector.tensor_tensor(z[:, 4:6], z[:, 1:2].broadcast_to([n, 2]), wdq[0:n, 0:2], ALU.mult)\
                    .then_inc(scale1_ready, 1)

            def gate_product(k):
                n = rows(ORDER[k])
                if k >= 2:
                    dve.wait_ge(lifted, 6 + 2 * k - 2)
                for half in range(2):
                    dve.wait_ge(gu_psum, 2 * k + half + 1)
                    dve.wait_ge(sg_ready, 2 * k + half + 1)
                    g = g2[k % 2][0:n, half * 512:(half + 1) * 512]
                    nc.vector.tensor_tensor(g, bank[3 + 2 * half][0:n, :],
                                            sg[0:n, k % 2, half * 512:(half + 1) * 512], ALU.mult)\
                        .then_inc(g2_ready, 1)

            def product_scale(k):
                t = ORDER[k]
                n = rows(t)
                z = q1[0:n, t, :]
                z5 = z[:, 5:6]
                dve.wait_ge(scale1_ready, k + 1)
                dve.wait_ge(g2_ready, 2 * k + 2)
                link(nc.vector.tensor_reduce(z[:, 0:1], g2[k % 2][0:n, :], AX_X, ALU.max,
                                             apply_absolute_value=True))
                link(nc.vector.tensor_scalar(z[:, 6:7], z[:, 0:1], z5, 1e-5, ALU.mult, ALU.max))
                link(nc.vector.reciprocal(z[:, 2:3], z[:, 6:7]))
                nc.vector.tensor_scalar(z[:, 3:4], z[:, 2:3], QMAX, z5, ALU.mult, ALU.mult)\
                    .then_inc(scale2_ready, 1)
                link(nc.vector.tensor_tensor(z[:, 7:8], z[:, 6:7], wdq[0:n, 2:3], ALU.mult))

            def quantise_last():
                h, z = slice(0, 512), q1[:, ORDER[TILES], :]
                dve.wait_ge(scale2_ready, TILES + 1)
                dve.wait_ge(g2q_ready, 2 * TILES - 1)
                link(nc.vector.tensor_scalar(g2m[:, h], g2[0][:, h], z[:, 3:4], MAGIC, ALU.mult, ALU.add))
                dve.wait_ge(g2T_psum, 2 * TILES - 3)
                nc.vector.tensor_scalar(g2q[:, 0, h], g2m[:, h], -MAGIC, None, ALU.add)\
                    .then_inc(g2q_last, 1)

            def copy_last_g2T():
                dve.wait_ge(g2T_psum, 2 * TILES + 2)
                dve.wait_ge(d_psum, TILES - 1)
                nc.vector.tensor_copy(g2T[:, 0, IC // 2:, :],
                                      bankb[2][:, 0:512].rearrange("p (c n) -> p c n", c=IC // 2))\
                    .then_inc(g2T_last, 1)

            def finish(k):
                t = ORDER[k]
                n = rows(t)
                dve.wait_ge(d_psum, k + 1)
                nc.vector.scalar_tensor_tensor(out=o_sb[0:n, t, :], in0=bank[DOWN_BANK[k]][0:n, 0:C],
                                               scalar=q1[0:n, t, 7:8], in1=h_sb[0:n, t, :],
                                               op0=ALU.mult, op1=ALU.add).then_inc(out_ready, 1)

            def clip(i, half):
                v = tern[("gate", "up", "down")[i]][:, half * INNER:(half + 1) * INNER]
                dve.wait_ge(rounded, 2 * i + half + 1)
                nc.vector.tensor_scalar(v, v, 1.0, -1.0, ALU.min, ALU.max).then_inc(tern_ready, 1)

            nc.vector.memset(ones[:, :], 1.0).then_inc(ones_ready, 1)
            nc.vector.memset(mhalf[:, :], -0.5).then_inc(const_ready, 1)
            dve.wait_ge(ld_eyef, 16)
            nc.vector.tensor_copy(eyeb[:, :], eyef[:, :]).then_inc(const_ready, 1)
            dve.wait_ge(ld_cls, 16)
            variance(0)
            norm1(0)
            nc.vector.memset(vb[:, 0:B // 2, :], 0.0).then_inc(vb_zero, 1)
            dve.wait_ge(ld_pos, 16)
            dve.wait_ge(ld_b, 16)
            link(nc.vector.tensor_tensor(posb[:, :], pos_sb[:, :], b_sb[:, :], ALU.add))
            variance(1)
            variance(2)
            norm1(1)
            variance(3)
            norm1(2)
            variance(4)
            norm1(3)
            norm1(4)
            dve.wait_ge(ld_tab, 48)
            rotate(0)
            dve.wait_ge(kc_psum, 1)
            nc.vector.tensor_copy(kcls[:, :], bank[7][:, 0:2]).then_inc(kc_copied, 1)
            rotate(1)
            dve.wait_ge(kc_copied, 1)
            dve.wait_ge(kb_zero, 1)
            for j in range(2):
                for g in range(G):
                    ps = slice(g * HD, (g + 1) * HD)
                    last = nc.vector.tensor_copy(kb[ps, j, :, g * S],
                                                 kcls[ps, j:j + 1].broadcast_to([HD, B]))
            last.then_inc(kcls_placed, 1)
            rotate(2)
            dve.wait_ge(vT_psum, 1)
            nc.vector.tensor_copy(vT[:, :], bank[7][:, 0:2]).then_inc(vT_ready, 1)
            rotate(3)
            rotate(4)
            rotate(5)
            rotate(6)
            dve.wait_ge(tot_psum, 1)
            nc.vector.tensor_scalar(wm[:, :], bank[7][:, 0:3], 1.0 / (C * INNER), 1e-5,
                                    ALU.mult, ALU.max).then_inc(wm_ready, 1)
            dve.wait_ge(wm_ready, 1)
            nc.vector.reciprocal(wscale[:, :], wm[:, :]).then_inc(wscale_ready, 1)
            link(nc.vector.tensor_scalar(wdq[:, :], wm[:, :], 1.0 / QMAX, None, ALU.mult))
            mask_scores(1)
            rotate(7)
            sum_exps(1)
            mask_scores(2)
            rotate(8)
            clip(0, 0)
            rotate(9)
            sum_exps(2)
            clip(0, 1)
            dve.wait_ge(ld_wo, 16)
            link(nc.vector.tensor_tensor(wo_sum[:, :, :], wo_sb[:, :, 0, :], wo_sb[:, :, 1, :], ALU.add))
            link(nc.vector.tensor_tensor(wo_sum[:, :, :], wo_sum[:, :, :], wo_sb[:, :, 2, :], ALU.add))
            nc.vector.tensor_tensor(wo_sum[:, :, :], wo_sum[:, :, :], wo_sb[:, :, 3, :], ALU.add)\
                .then_inc(wo_summed, 1)
            mask_scores(3)
            clip(1, 0)
            sum_exps(3)
            norm2(0)
            mask_scores(4)
            clip(1, 1)
            sum_exps(4)
            norm2(1)
            gate_product(0)
            product_scale(0)
            norm2(2)
            clip(2, 0)
            clip(2, 1)
            gate_product(1)
            product_scale(1)
            norm2(3)
            finish(0)
            gate_product(2)
            product_scale(2)
            finish(1)
            gate_product(3)
            product_scale(3)
            norm2(4)
            finish(2)
            finish(3)
            gate_product(4)
            product_scale(4)
            quantise_last()
            copy_last_g2T()
            finish(4)

        @block.scalar
        def _(act):
            def copy_yT(t):
                act.wait_ge(yT_psum, t + 1)
                nc.scalar.copy(yT[:, :, tcols(t)],
                               bank[4 + t % 2][:, 0:C].rearrange("p (c n) -> p c n", c=CC)[:, :, 0:rows(t)])\
                    .then_inc(yT_ready, 1)

            def copy_v(t):
                act.wait_ge(v_psum, t + 1)
                nc.scalar.copy(v_sb[0:rows(t), t, :], bank[6 + t % 2][0:rows(t), 0:C])\
                    .then_inc(v_ready, 1)

            def place_keys(half):
                act.wait_ge(kb_zero, 1)
                act.wait_ge(k_rotated, half + 1)
                bs = slice(half * B // 2, (half + 1) * B // 2)
                for j in range(2):
                    for g in range(G):
                        ps = slice(g * HD, (g + 1) * HD)
                        last = nc.scalar.copy(kb[ps, j, bs, g * S + 1:(g + 1) * S],
                                              kr[ps, j, :].rearrange("p (b n) -> p b n", n=N))
                last.then_inc(k_placed, 1)

            def lift_weights(i, half):
                v = raw[("gate", "up", "down")[i]][:, half * INNER:(half + 1) * INNER]
                nc.scalar.activation(v, v, ACT.Identity, scale=wscale[:, i:i + 1], bias=magic[:, 0:1])\
                    .then_inc(lifted, 1)

            def round_weights(i, half):
                name = ("gate", "up", "down")[i]
                cols = slice(half * INNER, (half + 1) * INNER)
                act.wait_ge(lifted, 2 * i + half + 1)
                nc.scalar.activation(tern[name][:, cols], raw[name][:, cols], ACT.Identity,
                                     bias=magic[:, 1:2]).then_inc(rounded, 1)

            def exps(t):
                act.wait_ge(shifted, t)
                nc.scalar.activation(ex[:, t - 1, :], sc[:, t - 1, :], ACT.Exp, scale=SCALE)\
                    .then_inc(exp_done, 1)

            def copy_pT(t):
                act.wait_ge(pT_psum, t)
                if t >= 3:
                    act.wait_ge(o_psum, t - 2)
                nc.scalar.copy(pT[:, t % 2, :], bank[6][0:GK, :]).then_inc(pT_ready, 1)

            def copy_oT(t):
                if t >= 3:
                    act.wait_ge(a_psum, ORDER.index(t - 2) + 1)
                for gp in range(2):
                    act.wait_ge(o_psum, 2 * t - 1 + gp)
                    nc.scalar.copy(
                        oT[:, t % 2, gp, :, :].rearrange("p r (b n) -> p b r n", n=N),
                        bank[gp][:, :].rearrange("p (b r n) -> p b r n", r=R, n=N))\
                        .then_inc(oT_ready, 1)

            def copy_xqT(k):
                act.wait_ge(xqT_psum, k + 1)
                if k >= 2:
                    act.wait_ge(gu_psum, 2 * k - 2)
                n = rows(ORDER[k])
                v = bankb[XQ_BANK[k]][:, 0:C].rearrange("p (c n) -> p c n", c=CC)
                nc.scalar.copy(xqT[:, k % 2, :, 0:n], v[:, :, 0:n]).then_inc(xqT_ready, 1)

            def silu(k):
                t = ORDER[k]
                n = rows(t)
                act.wait_ge(scale1_ready, k + 1)
                for half in range(2):
                    act.wait_ge(gu_psum, 2 * k + half + 1)
                    if k >= 2:
                        act.wait_ge(g2_ready, 2 * k + half - 3)
                    nc.scalar.activation(sg[0:n, k % 2, half * 512:(half + 1) * 512],
                                         bank[2 + 2 * half][0:n, :], ACT.Silu,
                                         scale=q1[0:n, t, 4:5]).then_inc(sg_ready, 1)

            def lift_product(k, halves=(0, 1)):
                t = ORDER[k]
                n = rows(t)
                act.wait_ge(scale2_ready, k + 1)
                for half in halves:
                    cols = slice(half * 512, (half + 1) * 512)
                    if k:
                        act.wait_ge(g2q_ready, 2 * k + half - 1)
                    nc.scalar.activation(g2m[0:n, cols], g2[k % 2][0:n, cols], ACT.Identity,
                                         scale=q1[0:n, t, 3:4], bias=magic[0:n, 0:1])\
                        .then_inc(lifted, 1)

            def copy_g2T(k, halves=(0, 1)):
                act.wait_ge(g2T_psum, 2 * k + len(halves))
                if k >= 2:
                    act.wait_ge(d_psum, k - 1)
                n = rows(ORDER[k])
                v = bankb[6].rearrange("p (c n) -> p c n", c=IC)
                for half in halves:
                    cs = slice(half * IC // 2, (half + 1) * IC // 2)
                    nc.scalar.copy(g2T[:, k % 2, cs, 0:n], v[:, cs, 0:n]).then_inc(g2T_ready, 1)

            act.dma_start(wtok_sb[:, 0, :], w_tok[0]).then_inc(ld_x[0], 16)
            act.dma_start(eyef[:, :], eye_f).then_inc(ld_eyef, 16)
            act.dma_start(h_sb[0:1, 0, :], cls_tok).then_inc(ld_cls, 16)
            act.dma_start(b_sb[:, :], tok_b.broadcast_to([P, C])).then_inc(ld_b, 16)
            copy_yT(0)
            copy_v(0)
            copy_yT(1)
            copy_yT(2)
            copy_v(1)
            copy_v(2)
            copy_yT(3)
            copy_yT(4)
            place_keys(0)
            copy_v(3)
            copy_v(4)
            for i, (name, s) in enumerate((("gate", ld_gate), ("up", ld_up), ("down", ld_down))):
                act.wait_ge(s, 16)
                nc.scalar.activation(tern[name][:, :], raw[name][:, :], ACT.Abs,
                                     accum_out=asum[:, i:i + 1]).then_inc(abs_done, 1)
            place_keys(1)
            act.wait_ge(const_ready, 4)
            act.wait_ge(wscale_ready, 1)
            act.wait_ge(abs_done, 3)
            lift_weights(0, 0)
            exps(1)
            lift_weights(0, 1)
            round_weights(0, 0)
            round_weights(0, 1)
            copy_pT(1)
            exps(2)
            lift_weights(1, 0)
            lift_weights(1, 1)
            copy_oT(1)
            round_weights(1, 0)
            exps(3)
            copy_pT(2)
            round_weights(1, 1)
            exps(4)
            copy_xqT(0)
            nc.scalar.activation(ahead[:, :], mask_sb[:, 0:1], ACT.Silu)
            copy_oT(2)
            lift_weights(2, 0)
            silu(0)
            copy_pT(3)
            copy_xqT(1)
            lift_weights(2, 1)
            round_weights(2, 0)
            silu(1)
            round_weights(2, 1)
            copy_oT(3)
            lift_product(0)
            copy_xqT(2)
            copy_g2T(0)
            lift_product(1)
            copy_pT(4)
            silu(2)
            copy_g2T(1)
            copy_oT(4)
            copy_xqT(3)
            lift_product(2)
            silu(3)
            copy_g2T(2)
            lift_product(3)
            copy_g2T(3)
            copy_xqT(4)
            silu(4)
            lift_product(4, halves=(1,))
            copy_g2T(4, halves=(0,))

        @block.gpsimd
        def _(pool):
            def inv_std(t, i, ready, done, k):
                n = rows(t)
                pool.wait_ge(ready, k + 1)
                nc.gpsimd.tensor_tensor(rstd[0:n, t, i, 1:2], rstd[0:n, t, i, 0:1], mhalf[0:n, :],
                                        ALU.pow).then_inc(done, 1)

            def combine(s):
                half, r = divmod(s, R + 1)
                pool.wait_ge(proj_read, s + 1)
                a, b = rc[:, s % 2, :, :], rs[:, s % 2, :, :]
                bs = slice(half * B // 2, (half + 1) * B // 2)
                for j, left, right, op in ((0, a[:, 0, :], b[:, 1, :], ALU.subtract),
                                           (1, b[:, 0, :], a[:, 1, :], ALU.add)):
                    last = nc.gpsimd.tensor_tensor(
                        qr[:, j, bs, r - 1, :], left.rearrange("p (b n) -> p b n", n=N),
                        right.rearrange("p (b n) -> p b n", n=N), op)
                last.then_inc(roped, 1)

            def shift(t):
                pool.wait_ge(smax_ready, t)
                v = sc[:, t - 1, :].rearrange("p (a k) -> p a k", k=S)
                nc.gpsimd.tensor_tensor(v, v, smax[:, t - 1, :].unsqueeze(2)
                                        .broadcast_to([P, PAIRS * G, S]), ALU.subtract)\
                    .then_inc(shifted, 1)

            def normalise(t):
                pool.wait_ge(srec_ready, t)
                v = ex[:, t - 1, :].rearrange("p (a k) -> p a k", k=S)
                nc.gpsimd.tensor_tensor(v, v, srec[:, t - 1, :].unsqueeze(2)
                                        .broadcast_to([P, PAIRS * G, S]), ALU.mult)\
                    .then_inc(probs_ready, 1)

            def inv_std2(k):
                inv_std(ORDER[k], 1, var2_ready, rstd2_ready, k)

            def round_product(k, halves=(0, 1)):
                n = rows(ORDER[k])
                for half in halves:
                    cols = slice(half * 512, (half + 1) * 512)
                    if k >= 2:
                        pool.wait_ge(g2T_psum, 2 * k + half - 3)
                    pool.wait_ge(lifted, 6 + 2 * k + halves.index(half) + 1)
                    nc.gpsimd.tensor_scalar(g2q[0:n, k % 2, cols], g2m[0:n, cols], 1.0, -MAGIC,
                                            ALU.mult, ALU.add).then_inc(g2q_ready, 1)

            nc.gpsimd.memset(kb[:, :, :, :], 0.0).then_inc(kb_zero, 1)
            nc.gpsimd.memset(magic[:, 0:1], MAGIC).then_inc(const_ready, 1)
            nc.gpsimd.memset(magic[:, 1:2], -MAGIC).then_inc(const_ready, 1)
            pool.wait_ge(const_ready, 4)
            inv_std(0, 0, var_ready, rstd_ready, 0)
            nc.gpsimd.memset(vb[:, B // 2:B, :], 0.0).then_inc(vb_zero, 1)
            for t in PATCH:
                inv_std(t, 0, var_ready, rstd_ready, t)
            for s in (1, 2, 3, 4, 6):
                combine(s)
            shift(1)
            normalise(1)
            combine(7)
            shift(2)
            combine(8)
            combine(9)
            normalise(2)
            shift(3)
            normalise(3)
            inv_std2(0)
            shift(4)
            normalise(4)
            inv_std2(1)
            inv_std2(2)
            round_product(0)
            round_product(1)
            inv_std2(3)
            round_product(2)
            round_product(3)
            inv_std2(4)
            round_product(4, halves=(1,))


def shape_constants():
    import numpy as np
    inv = (1.0 / np.float32(10000.0) ** (np.arange(0, D, 2, dtype=np.float32) / np.float32(D)))
    ang = np.arange(1, S, dtype=np.float32)[None, :] * inv.astype(np.float32)[:, None]
    cos_t = np.tile(np.cos(ang).astype(np.float32), (G, 1))
    sin_t = np.tile(np.sin(ang).astype(np.float32), (G, 1))
    q = np.arange(P)[:, None] % N + 1
    mask_t = np.where(np.arange(S)[None, :] <= q, 0.0, MASKED).astype(np.float32)
    return {"cos_t": cos_t, "sin_t": sin_t, "mask_t": mask_t,
            "eye_f": np.eye(P, dtype=np.float32)}


def kernel(**inputs):
    import numpy as np
    import concourse.bacc as bacc
    from concourse.bass_utils import run_bass_kernel_spmd

    a = {k: np.asarray(v) for k, v in inputs.items()}
    ps = 16
    lay = {
        "xT": a["x"].reshape(B, 3, 4, ps, 4, ps).transpose(1, 3, 5, 0, 2, 4).reshape(FC, P, TOK),
        "w_tok": a["L0_tok_W"].T.reshape(FC, P, C),
        "tok_b": a["L0_tok_b"].reshape(1, C),
        "pos": np.tile(a["L0_tok_pos_emb"], (TI, 1)),
        "cls_tok": a["cls_tok"].reshape(1, C),
        "wq": a["L0_attn_Wq"].reshape(CC, P, G, R, HD, 2).transpose(1, 0, 3, 5, 2, 4)
                             .reshape(P, CC, R, 2, P),
        "wk": a["L0_attn_Wk"].reshape(CC, P, G, HD, 2).transpose(1, 0, 4, 2, 3).reshape(P, CC, 2, P),
        "wv": a["L0_attn_Wv"].reshape(CC, P, C).transpose(1, 0, 2),
        "wo": a["L0_attn_Wo"].reshape(2, 2, R, D, C).transpose(1, 3, 0, 2, 4).reshape(P, 2, R, C),
        "w_gate": a["L0_ffn_w_gate"].T.reshape(CC, P, INNER).transpose(1, 0, 2).reshape(P, 2 * INNER),
        "w_up": a["L0_ffn_w_up"].T.reshape(CC, P, INNER).transpose(1, 0, 2).reshape(P, 2 * INNER),
        "w_down": a["L0_ffn_w_down"].T.reshape(IC, P, C).transpose(1, 0, 2).reshape(P, 2 * INNER),
    }
    lay.update(shape_constants())

    nc = bacc.Bacc("TRN2", target_bir_lowering=False, num_devices=1)
    arrays, args = {}, {}
    for name, v in lay.items():
        v = np.ascontiguousarray(v)
        arrays[f"in_{name}"] = v
        args[name] = nc.dram_tensor(f"in_{name}", v.shape, mybir.dt.from_np(v.dtype),
                                    kind="ExternalInput").ap()
    out = nc.dram_tensor("out_0", (B, S, C), F32, kind="ExternalOutput").ap()
    build(nc, out=out, **args)
    r = run_bass_kernel_spmd(nc, [arrays], core_ids=[0])
    return r.results[0]["out_0"]
```
